# Optimizing a Trainium2 kernel written in Bass

```python
import numpy as np
import jax
import jax.numpy as jnp

def _softmax(x, axis=-1):
    return jax.nn.softmax(x, axis=axis)

def _gelu(x):
    return jax.nn.gelu(x, approximate=True)

def _silu(x):
    return jax.nn.silu(x)

def _sigmoid(x):
    return jax.nn.sigmoid(x)

def _layernorm(x, axis=-1, eps=1e-05):
    m = jnp.mean(x, axis=axis, keepdims=True)
    v = jnp.var(x, axis=axis, keepdims=True)
    return (x - m) / jnp.sqrt(v + eps)

def _scatter_add(tgt, idx, src, axis=0):
    return tgt.at[idx].add(src)

def _segment_sum(src, seg, n):
    return jax.ops.segment_sum(src, seg, n)
kernel_name = 'mk_seq_postln_d2_jaxref_r8_0048f4'

def setup_inputs(seed: int=0):
    np.random.seed(seed)
    _w = jnp.asarray

    def _L0_attn_setup():
        import math
        import jax, jax.numpy as jnp
        import numpy as np
        B, S, D, H, DH = (2, 256, 128, 16, 64)
        INNER = H * DH

        def _l2norm(t):
            n = jnp.linalg.norm(t, axis=-1, keepdims=True)
            return t / jnp.maximum(n, 1e-12)
        key = jax.random.key(seed)
        k0, k1, k2, k3 = jax.random.split(key, 4)
        x = jax.random.normal(k0, (B, S, D), dtype=jnp.float32)
        w_q = jax.random.normal(k1, (D, INNER), dtype=jnp.float32) * 0.02
        w_kv = jax.random.normal(k2, (D, 2 * INNER), dtype=jnp.float32) * 0.02
        w_out = jax.random.normal(k3, (INNER, D), dtype=jnp.float32) * 0.02
        b_out = jnp.zeros((D,), dtype=jnp.float32)
        scale_init = -math.log(math.log2(S ** 2 - S))
        scale = jnp.full((1, H, 1, 1), scale_init, dtype=jnp.float32)
        return {'x': x, 'w_q': w_q, 'w_kv': w_kv, 'w_out': w_out, 'b_out': b_out, 'scale': scale}
    _L0_attn_in = _L0_attn_setup()

    def _L0_ffn_setup():
        import jax, jax.numpy as jnp
        import numpy as np
        B, S, H = (2, 256, 128)
        E, I, K = (8, 512, 2)

        def _moe_forward(x, gate_w, wg, wu, wd):
            b, s, h = x.shape
            x_flat = x.reshape(-1, h)
            logits = x_flat @ gate_w.T
            top_v, top_i = jax.lax.top_k(logits, K)
            probs = jax.nn.softmax(top_v.astype(jnp.float32), axis=-1).astype(logits.dtype)
            one_hot = jax.nn.one_hot(top_i, E, dtype=probs.dtype)
            combine = jnp.einsum('tk,tke->et', probs, one_hot)

            def body(acc, ws):
                wge, wue, wde, we = ws
                hidden = jax.nn.silu(x_flat @ wge.T) * (x_flat @ wue.T)
                return (acc + we[:, None] * (hidden @ wde.T), None)
            out, _ = jax.lax.scan(body, jnp.zeros_like(x_flat), (wg, wu, wd, combine))
            return out.reshape(b, s, h)
        key = jax.random.key(seed)
        ks = jax.random.split(key, 5)
        scale_h = 1.0 / np.sqrt(H)
        scale_i = 1.0 / np.sqrt(I)
        x = jax.random.normal(ks[0], (B, S, H), dtype=jnp.float32)
        gate_w = jax.random.normal(ks[1], (E, H), dtype=jnp.float32) * scale_h
        wg = jax.random.normal(ks[2], (E, I, H), dtype=jnp.float32) * scale_h
        wu = jax.random.normal(ks[3], (E, I, H), dtype=jnp.float32) * scale_h
        wd = jax.random.normal(ks[4], (E, H, I), dtype=jnp.float32) * scale_i
        return {'x': x, 'gate_w': gate_w, 'wg': wg, 'wu': wu, 'wd': wd}
    _L0_ffn_in = _L0_ffn_setup()

    def _L1_attn_setup():
        import jax, jax.numpy as jnp
        import numpy as np
        DT_MIN, DT_MAX = (0.001, 0.1)
        BSZ, SEQ, DM, DS = (8, 256, 128, 16)

        def _depthwise_conv(x, conv_w, conv_b):
            xc = jnp.transpose(x, (0, 2, 1))
            y = jax.lax.conv_general_dilated(xc, conv_w, window_strides=(1,), padding=[(1, 1)], feature_group_count=xc.shape[1], dimension_numbers=('NCH', 'OIH', 'NCH'))
            y = y + conv_b[None, :, None]
            return jnp.transpose(y, (0, 2, 1))
        key = jax.random.key(seed)
        ks = jax.random.split(key, 8)
        x = jax.random.normal(ks[0], (BSZ, SEQ, DM), jnp.float32)
        a_log = jax.random.normal(ks[1], (DM, DS), jnp.float32) * -0.5
        b = jax.random.normal(ks[2], (DM, DS), jnp.float32) * 0.02
        c = jax.random.normal(ks[3], (DM, DS), jnp.float32) * 0.02
        dt_w = jax.random.normal(ks[4], (DM, DM), jnp.float32) * (1.0 / np.sqrt(DM))
        dt_b = jnp.zeros((DM,), jnp.float32)
        conv_w = jax.random.normal(ks[5], (DM, 1, 3), jnp.float32) * (1.0 / np.sqrt(3.0))
        conv_b = jnp.zeros((DM,), jnp.float32)
        return {'x': x, 'a_log': a_log, 'b': b, 'c': c, 'dt_w': dt_w, 'dt_b': dt_b, 'conv_w': conv_w, 'conv_b': conv_b}
    _L1_attn_in = _L1_attn_setup()

    def _L1_ffn_setup():
        import jax, jax.numpy as jnp
        import numpy as np
        TOP_K = 2

        def _mlp(x, w_fc, w_proj):
            return jnp.square(jax.nn.relu(x @ w_fc.T)) @ w_proj.T
        key = jax.random.key(seed)
        ks = jax.random.split(key, 6)
        B, S, D, E = (4, 256, 128, 8)
        d_ff = 4 * D
        x = jax.random.normal(ks[0], (B, S, D), dtype=jnp.float32)
        router_w = jax.random.normal(ks[1], (E, D), dtype=jnp.float32) * 0.02
        w_fc = jax.random.normal(ks[2], (E, d_ff, D), dtype=jnp.float32) * 0.02
        w_proj = jax.random.normal(ks[3], (E, D, d_ff), dtype=jnp.float32) * 0.02
        shared_fc = jax.random.normal(ks[4], (d_ff, D), dtype=jnp.float32) * 0.02
        shared_proj = jax.random.normal(ks[5], (D, d_ff), dtype=jnp.float32) * 0.02
        return {'x': x, 'router_w': router_w, 'w_fc': w_fc, 'w_proj': w_proj, 'shared_fc': shared_fc, 'shared_proj': shared_proj}
    _L1_ffn_in = _L1_ffn_setup()
    _d = {'L0_attn_x': _L0_attn_in['x'], 'L0_attn_w_q': _L0_attn_in['w_q'], 'L0_attn_w_kv': _L0_attn_in['w_kv'], 'L0_attn_w_out': _L0_attn_in['w_out'], 'L0_attn_b_out': _L0_attn_in['b_out'], 'L0_attn_scale': _L0_attn_in['scale'], 'L0_ffn_gate_w': _L0_ffn_in['gate_w'], 'L0_ffn_wg': _L0_ffn_in['wg'], 'L0_ffn_wu': _L0_ffn_in['wu'], 'L0_ffn_wd': _L0_ffn_in['wd'], 'L1_attn_a_log': _L1_attn_in['a_log'], 'L1_attn_b': _L1_attn_in['b'], 'L1_attn_c': _L1_attn_in['c'], 'L1_attn_dt_w': _L1_attn_in['dt_w'], 'L1_attn_dt_b': _L1_attn_in['dt_b'], 'L1_attn_conv_w': _L1_attn_in['conv_w'], 'L1_attn_conv_b': _L1_attn_in['conv_b'], 'L1_ffn_router_w': _L1_ffn_in['router_w'], 'L1_ffn_w_fc': _L1_ffn_in['w_fc'], 'L1_ffn_w_proj': _L1_ffn_in['w_proj'], 'L1_ffn_shared_fc': _L1_ffn_in['shared_fc'], 'L1_ffn_shared_proj': _L1_ffn_in['shared_proj']}
    _x0 = _d['L0_attn_x']
    _d['L0_attn_x'] = jax.random.normal(jax.random.fold_in(jax.random.key(seed), 1), (2, 1024, 128), dtype=_x0.dtype)
    del _x0
    return _d

def reference(L0_attn_x, L0_attn_w_q, L0_attn_w_kv, L0_attn_w_out, L0_attn_b_out, L0_attn_scale, L0_ffn_gate_w, L0_ffn_wg, L0_ffn_wu, L0_ffn_wd, L1_attn_a_log, L1_attn_b, L1_attn_c, L1_attn_dt_w, L1_attn_dt_b, L1_attn_conv_w, L1_attn_conv_b, L1_ffn_router_w, L1_ffn_w_fc, L1_ffn_w_proj, L1_ffn_shared_fc, L1_ffn_shared_proj):

    def _L0_attn_ref(x, w_q, w_kv, w_out, b_out, scale):
        import math
        import jax, jax.numpy as jnp
        import numpy as np
        B, S, D, H, DH = (2, 256, 128, 16, 64)
        INNER = H * DH

        def _l2norm(t):
            n = jnp.linalg.norm(t, axis=-1, keepdims=True)
            return t / jnp.maximum(n, 1e-12)
        b, s, _ = x.shape
        h = scale.shape[1]
        q = (x @ w_q).reshape(b, s, h, -1).transpose(0, 2, 1, 3)
        kv = x @ w_kv
        k, v = jnp.split(kv, 2, axis=-1)
        k = k.reshape(b, s, h, -1).transpose(0, 2, 1, 3)
        v = v.reshape(b, s, h, -1).transpose(0, 2, 1, 3)
        q = _l2norm(q) * jnp.exp(scale)
        k = _l2norm(k)
        sim = jnp.einsum('bhid,bhjd->bhij', q, k)
        attn = jax.nn.softmax(sim, axis=-1)
        out = jnp.einsum('bhij,bhjd->bhid', attn, v)
        out = out.transpose(0, 2, 1, 3).reshape(b, s, h * out.shape[-1])
        return out @ w_out + b_out

    def _L0_ffn_ref(x, gate_w, wg, wu, wd):
        import jax, jax.numpy as jnp
        import numpy as np
        B, S, H = (2, 256, 128)
        E, I, K = (8, 512, 2)

        def _moe_forward(x, gate_w, wg, wu, wd):
            b, s, h = x.shape
            x_flat = x.reshape(-1, h)
            logits = x_flat @ gate_w.T
            top_v, top_i = jax.lax.top_k(logits, K)
            probs = jax.nn.softmax(top_v.astype(jnp.float32), axis=-1).astype(logits.dtype)
            one_hot = jax.nn.one_hot(top_i, E, dtype=probs.dtype)
            combine = jnp.einsum('tk,tke->et', probs, one_hot)

            def body(acc, ws):
                wge, wue, wde, we = ws
                hidden = jax.nn.silu(x_flat @ wge.T) * (x_flat @ wue.T)
                return (acc + we[:, None] * (hidden @ wde.T), None)
            out, _ = jax.lax.scan(body, jnp.zeros_like(x_flat), (wg, wu, wd, combine))
            return out.reshape(b, s, h)
        return _moe_forward(x, gate_w, wg, wu, wd)

    def _L1_attn_ref(x, a_log, b, c, dt_w, dt_b, conv_w, conv_b):
        import jax, jax.numpy as jnp
        import numpy as np
        DT_MIN, DT_MAX = (0.001, 0.1)
        BSZ, SEQ, DM, DS = (8, 256, 128, 16)

        def _depthwise_conv(x, conv_w, conv_b):
            xc = jnp.transpose(x, (0, 2, 1))
            y = jax.lax.conv_general_dilated(xc, conv_w, window_strides=(1,), padding=[(1, 1)], feature_group_count=xc.shape[1], dimension_numbers=('NCH', 'OIH', 'NCH'))
            y = y + conv_b[None, :, None]
            return jnp.transpose(y, (0, 2, 1))
        Bn, N, C = x.shape
        D = a_log.shape[1]
        xf = _depthwise_conv(x, conv_w, conv_b)
        dt = jax.nn.sigmoid(xf @ dt_w.T + dt_b) * (DT_MAX - DT_MIN) + DT_MIN
        A = -jax.nn.softplus(a_log)

        def step(s, inp):
            xt, dtt = inp
            expA = jnp.exp(dtt[..., None] * A)
            s = expA * s + (dtt * xt)[..., None] * b
            y = jnp.einsum('bcd,cd->bc', s, c)
            return (s, y)
        s0 = jnp.zeros((Bn, C, D), x.dtype)
        xs = (jnp.transpose(xf, (1, 0, 2)), jnp.transpose(dt, (1, 0, 2)))
        _, ys = jax.lax.scan(step, s0, xs)
        return jnp.transpose(ys, (1, 0, 2))

    def _L1_ffn_ref(x, router_w, w_fc, w_proj, shared_fc, shared_proj):
        import jax, jax.numpy as jnp
        import numpy as np
        TOP_K = 2

        def _mlp(x, w_fc, w_proj):
            return jnp.square(jax.nn.relu(x @ w_fc.T)) @ w_proj.T
        B, S, D = x.shape
        E = router_w.shape[0]
        T = B * S
        flat = x.reshape(T, D)
        logits = flat @ router_w.T
        probs = jax.nn.softmax(logits.astype(jnp.float32), axis=-1)
        topk_p, topk_i = jax.lax.top_k(probs, TOP_K)
        topk_w = (topk_p / jnp.maximum(topk_p.sum(-1, keepdims=True), 1e-09)).astype(flat.dtype)
        combine = jnp.zeros((T, E), dtype=flat.dtype)
        combine = combine.at[jnp.arange(T)[:, None], topk_i].add(topk_w)
        out = jnp.zeros_like(flat)
        for e in range(E):
            out = out + _mlp(flat, w_fc[e], w_proj[e]) * combine[:, e:e + 1]
        out = out + _mlp(flat, shared_fc, shared_proj)
        return out.reshape(B, S, D)
    x = L0_attn_x
    x = _layernorm(x + _L0_attn_ref(x, L0_attn_w_q, L0_attn_w_kv, L0_attn_w_out, L0_attn_b_out, L0_attn_scale), axis=-1)
    x = _layernorm(x + _L0_ffn_ref(x, L0_ffn_gate_w, L0_ffn_wg, L0_ffn_wu, L0_ffn_wd), axis=-1)
    x = _layernorm(x + _L1_attn_ref(x, L1_attn_a_log, L1_attn_b, L1_attn_c, L1_attn_dt_w, L1_attn_dt_b, L1_attn_conv_w, L1_attn_conv_b), axis=-1)
    x = _layernorm(x + _L1_ffn_ref(x, L1_ffn_router_w, L1_ffn_w_fc, L1_ffn_w_proj, L1_ffn_shared_fc, L1_ffn_shared_proj), axis=-1)
    return x

_drawn_inputs = setup_inputs


def setup_inputs(seed=0):
    import zlib

    import numpy as np

    out = dict(_drawn_inputs(seed))
    spreads = {'L0_attn_b_out': (0.0, 0.1),
     'L0_attn_scale': (-2.772235631942749, 0.6),
     'L1_attn_dt_b': (0.0, 0.8),
     'L1_attn_conv_b': (0.0, 0.8)}
    factors = {'L0_attn_w_q': 8.0,
     'L0_attn_w_out': 2.725,
     'L1_attn_a_log': 8.0,
     'L1_attn_b': 8.0,
     'L1_attn_c': 8.0,
     'L1_attn_dt_w': 8.0,
     'L1_attn_conv_w': 8.0,
     'L1_ffn_router_w': 3.235,
     'L1_ffn_w_fc': 3.11,
     'L1_ffn_w_proj': 2.85}
    for name, (base, spread) in spreads.items():
        noise = np.random.default_rng([zlib.crc32(name.encode()), seed]).standard_normal(out[name].shape)
        drawn = base * np.exp(spread * noise) if base else spread * noise
        out[name] = jnp.asarray(drawn.astype(out[name].dtype))
    for name, factor in factors.items():
        out[name] = (out[name] * factor).astype(out[name].dtype)
    return out
```

```python
import concourse.bass as bass
from concourse import mybir
from contextlib import ExitStack

F32 = mybir.dt.float32
F16 = mybir.dt.float16
BF16 = mybir.dt.bfloat16
U32 = mybir.dt.uint32
ALU = mybir.AluOpType
ACT = mybir.ActivationFunctionType
AX = mybir.AxisListType.X

P = 128
B, S, D = 2, 1024, 128
T = B * S
NT = T // P
H, DH = 16, 64
QKV = 3 * DH
E = 8
FF = 512
NC = FF // P
EPS = 1e-5


def high(ap):
    return ap.bitcast(BF16)


def wait(eng, sem, count):
    if not isinstance(count, int) or count > 0:
        eng.wait_ge(sem, count)


SLOTS = 16
QW = 256
KT = 4
PB = 4
LAG = 2
PJ = 8
VW = 130
STK = 5 * DH
WCH = 4


TAIL = 32
POOL_LO = (4, 13, 15)
GROUP_AT = (0, 3, 6, 8)


def low_count(i, s, pool):
    mine = [k for k in range(SLOTS) if (k in POOL_LO) == pool]
    return 2 * len(mine) * i + s // SLOTS * len(mine) + sum(k <= s % SLOTS for k in mine)


def proj_slot(j):
    return GROUP_AT[j // 2] + j % 2


def tp_slot(j):
    return 7 + j


def at_slot(place, s, n=PJ):
    return next((j for j in range(n) if place(j) == s), None)


def before(place, s, n=PJ):
    return sum(place(j) < s for j in range(n))


def turn_slot(u):
    return 31 + u


def out_slot(u):
    return (42, 43, 45, 47, 58, 59, 61, 63)[u]


def out_unit(s, place):
    for back in (0, 1):
        if (u := at_slot(place, s + 2 * SLOTS * back)) is not None:
            return back, u
    return None


def out_before(s, place):
    return before(place, s) + before(place, s + 2 * SLOTS) - PJ


class Semaphores:

    def __init__(self, nc, tag):
        self.nc, self.tag, self.made = nc, tag, []

    def __call__(self, name):
        self.made.append(self.nc.alloc_semaphore(name=f"{name}_{self.tag}"))
        return self.made[-1]

    def end(self):
        self.nc.clear_and_free_semaphores(self.made)
        self.nc.all_engine_barrier()


def attention(nc, ctx, io, t):
    es = ExitStack()
    sem = Semaphores(nc, "at")

    def sb(name, shape, dt):
        return es.enter_context(nc.sbuf_tensor(name, shape, dt))

    def ps(name, shape, dt):
        return es.enter_context(nc.psum_tensor(name, shape, dt))

    with es:
        w_hi = sb("w_hi", [P, H * QKV], F16)
        w_lo = sb("w_lo", [P, H * QKV], F16)
        xT_hi = sb("xT_hi", [P, T], F16)
        xT_lo = sb("xT_lo", [P, T], F16)
        wo = sb("wo", [P, H // 2 * D], F32)
        esc = sb("esc", [P, H], F32)
        nesc = sb("nesc", [P, H], F32)
        scl = sb("scl", [P, H], F32)
        cur_esc = sb("cur_esc", [P, 2], F32)
        cur_nesc = sb("cur_nesc", [P, 2], F32)
        raw = sb("raw", [P, 4, 4, QKV], F32)
        sq = sb("sq", [P, 2, 4, 2, DH], F32)
        ss = sb("ss", [P, 2, 4, 2], F32)
        rn = sb("rn", [P, 2, 4, 2], F32)
        nrm = sb("nrm", [P, 2, 4, 2, DH], F32)
        stk = sb("stk", [P, 4, 4, STK], F16)
        QK = sb("QK", [P, 2, 3, T], F16)
        V = sb("V", [P, 2, NT, VW], F16)
        Pr = sb("Pr", [P, PB, KT, QW], F32)
        Pl = sb("Pl", [P, PB, KT, QW], F16)
        rden = sb("rden", [P, 4, 2], F32)
        Or = sb("Or", [P, 4, 258], F32)
        osum = sb("osum", [P, 2, 2, DH], F32)
        Ob = sb("Ob", [P, NT, 2 * DH], F32)
        OT = sb("OT", [P, PJ, 2, P], F32)
        half = sb("mhalf", [P, 1], F32)
        w_f32 = QK[:, 1, :, :].rearrange("p k t -> p (k t)").bitcast(F32)
        xT_f32 = Pr[:, 0:2, :, :].rearrange("p a b c -> p (a b c)")
        ss2 = sb("ss2", [P, 2, 4, 2], F32)

        SC = [ps(f"SC{i}", [P, KT, QW], F32) for i in range(2)]
        OP = [ps(f"OP{i}", [P, 512], F32) for i in range(2)]
        M0 = ps("M0", [P, 512], F32)
        M1 = ps("M1", [P, 512], F32)

        s_ld = {k: sem("s_ld_" + k) for k in ("x", "w", "xt", "wo", "scl")}
        s_init = sem("s_init")
        s_wsp = sem("s_wsp")
        s_xsp = sem("s_xsp")
        s_esc = sem("s_esc")
        s_nesc = sem("s_nesc")
        s_cur = sem("s_cur")
        s_sc = sem("s_sc")
        s_ex = sem("s_ex")
        s_pl = sem("s_pl")
        s_plp = sem("s_plp")
        s_av = sem("s_av")
        s_ob = sem("s_ob")
        s_dv = sem("s_dv")
        s_pj = sem("s_pj")
        s_raw = sem("s_raw")
        s_sq = sem("s_sq")
        s_ss = sem("s_ss")
        s_cl = sem("s_cl")
        s_pw = sem("s_pw")
        s_rn = sem("s_rn")
        s_nrm = sem("s_nrm")
        s_vh = sem("s_vh")
        s_vl = sem("s_vl")
        s_hi = sem("s_hi")
        s_dup = sem("s_dup")
        s_lo = sem("s_lo")
        s_tp = sem("s_tp")
        s_o = sem("s_o")
        s_os = sem("s_os")
        s_ot = sem("s_ot")
        s_ote = sem("s_ote")
        s_y = sem("s_y")
        s_acc = sem("s_acc")
        s_xb = sem("s_xb")
        s_half = sem("s_half")
        s_tpd = sem("s_tpd")
        s_tpa = sem("s_tpa")
        block = es.enter_context(nc.Block())

        def heads(eng, emit):
            for s in range(2 * SLOTS):
                emit(0, s)
            with eng.Fori(1, H // 2 - 1) as i:
                for s in range(2 * SLOTS):
                    emit(i, s)
            for s in range(2 * SLOTS):
                emit(H // 2 - 1, s)
            for s in range(TAIL):
                emit(H // 2, s)

        def ended(i):
            return isinstance(i, int) and i == H // 2

        def prepares(i, s):
            return not (isinstance(i, int) and 2 * i + s // SLOTS >= H - 1)

        def started(i, back):
            return not (isinstance(i, int) and i - back < 0)

        def exists(i, back):
            return started(i, back) and not (ended(i) and not back)

        @block.sync
        def _(eng):
            eng.dma_start(xT_f32, io["xT"]).then_inc(s_ld["xt"], 16)
            eng.dma_start(w_f32, io["wqkv"]).then_inc(s_ld["w"], 16)
            eng.dma_start(scl[:, :], io["scale"].partition_broadcast(P)).then_inc(s_ld["scl"], 16)
            eng.dma_start(wo[:, :], io["wout"]).then_inc(s_ld["wo"], 16)
            eng.dma_start(t["x"][:, :, :], io["x"].rearrange("(t p) d -> p t d", p=P)).then_inc(s_ld["x"], 16)
            eng.dma_start(t["bout"][:, :], io["b_out"].partition_broadcast(P)).then_inc(s_ld["x"], 16)

        @block.tensor
        def _(eng):
            ident16, ident32 = t["ident16"], t["ident32"]

            def m0_free(h, j, i, s):
                wait(eng, s_sq, 8 * h + j)
                wait(eng, s_acc, 8 * i + out_before(s, out_slot))

            def m1_free(h, j, i, s):
                wait(eng, s_tpd, 4 * h + (j + 1) // 2)
                wait(eng, s_tpa, 4 * h + j // 2)
                wait(eng, s_ote, 8 * i + out_before(s, turn_slot))

            def proj(h, j):
                for r in range(2):
                    tile = 2 * j + r
                    out = M0[:, QKV * r:QKV * r + QKV]
                    hi, lo = xT_hi[:, P * tile:P * tile + P], xT_lo[:, P * tile:P * tile + P]
                    wh, wl = w_hi[:, bass.ds(QKV * h, QKV)], w_lo[:, bass.ds(QKV * h, QKV)]
                    eng.matmul(out, hi, wh, start=True, stop=False)
                    eng.matmul(out, hi, wl, start=False, stop=False)
                    mm = eng.matmul(out, lo, wh, start=False, stop=True)
                mm.then_inc(s_pj, 1)

            def transposes(h, j):
                g = j // 2
                wait(eng, s_hi, 4 * h + g + 1)
                wait(eng, s_dup, 4 * h + g + 1)
                wait(eng, s_lo, 4 * h + g + 1)
                m1 = M1[:, :].bitcast(F16)
                for kind in range(3):
                    at = (0, 2 * DH, 3 * DH)[kind]
                    for r in range(2):
                        mm = eng.transpose(m1[:, (2 * kind + r) * P:(2 * kind + r + 1) * P],
                                           stk[:, g, 2 * (j % 2) + r, at:at + P], ident16[:, :])
                mm.then_inc(s_tp, 1)

            def scores(i, s):
                n, h, b = 32 * i + s, 2 * i + s // SLOTS, s // SLOTS
                s %= SLOTS
                bat, q, kh = s // 8, s % 8 // 2, s % 2
                if s == 0:
                    wait(eng, s_tpd, 4 * h + 4)
                    wait(eng, s_tpa, 4 * h + 4)
                wait(eng, s_ex, n - 1)
                for kt in range(KT):
                    key = bat * S + (kh * KT + kt) * P
                    rhs = QK[:, b, 0, bat * S + q * QW:bat * S + q * QW + QW]
                    out = SC[s % 2][:, kt, :]
                    eng.matmul(out, QK[:, b, 1, key:key + P], rhs, start=True, stop=False)
                    mm = eng.matmul(out, QK[:, b, 2, key:key + P], rhs, start=False, stop=True)
                mm.then_inc(s_sc, 1)

            def av(i, s):
                n, h, b = 32 * i + s, 2 * i + s // SLOTS, s // SLOTS
                s %= SLOTS
                bat, kh, u = s // 8, s % 2, s // 2
                pool = s in POOL_LO
                wait(eng, s_plp if pool else s_pl, low_count(i, s + SLOTS * b, pool))
                if s == 0:
                    wait(eng, s_vh, 4 * h + 4)
                    wait(eng, s_vl, 4 * h + 4)
                if kh == 0:
                    wait(eng, s_ob, 16 * i + 8 * b + u - 1)
                for kt in range(KT):
                    tile = bat * 8 + kh * KT + kt
                    for r in range(2):
                        hi = high(Pr[:, s % PB, kt, P * r:P * r + P])[:, 1::2]
                        lo = Pl[:, s % PB, kt, P * r:P * r + P]
                        at = 129 * r
                        first = kh == 0 and kt == 0 and r == 0
                        last = kh == 1 and kt == KT - 1 and r == 1
                        eng.matmul(OP[u % 2][:, at:at + 129], hi, V[:, b, tile, 0:129],
                                   start=first, stop=False, skip_group_check=True)
                        mm = eng.matmul(OP[u % 2][:, at:at + 65], lo, V[:, b, tile, 0:65],
                                        start=False, stop=last, skip_group_check=True)
                mm.then_inc(s_av, 1)

            def out_transposes(i, u):
                wait(eng, s_o, 16 * i + 8 + u + 1)
                for r in range(2):
                    mm = eng.transpose(M1[:, P * r:P * r + P], Ob[:, 2 * u + r, :], ident32[:, :])
                mm.then_inc(s_ot, 1)

            def out_product(i, u):
                wait(eng, s_ote, 8 * i + u + 1)
                for r in range(2):
                    mm = eng.matmul(M0[:, P * r:P * r + P], OT[:, u, r, :],
                                    wo[:, bass.ds(D * i, D)], start=True, stop=True)
                mm.then_inc(s_y, 1)

            def slot(i, s):
                h, sh = 2 * i + s // SLOTS, s % SLOTS
                pj, tp = before(proj_slot, sh), before(tp_slot, sh)
                if not prepares(i, s):
                    pj, tp = (0, 0) if ended(i) or s >= SLOTS else (pj, tp)
                nh = H if not prepares(i, s) else h + 1
                if not ended(i):
                    scores(i, s)
                if s >= LAG and not ended(i):
                    av(i, s - LAG)
                elif s < LAG and started(i, 1):
                    av(i - 1, s + 2 * SLOTS - LAG)
                if (x := out_unit(s, turn_slot)) and exists(i, x[0]):
                    m1_free(nh, tp, i, s)
                    out_transposes(i - x[0], x[1])
                if (x := out_unit(s, out_slot)) and exists(i, x[0]):
                    m0_free(nh, pj, i, s)
                    out_product(i - x[0], x[1])
                if prepares(i, s):
                    if (j := at_slot(proj_slot, sh)) is not None:
                        m0_free(h + 1, j, i, s)
                        proj(h + 1, j)
                    if (j := at_slot(tp_slot, sh)) is not None:
                        m1_free(h + 1, j, i, s)
                        transposes(h + 1, j)

            eng.wait_ge(s_wsp, 2 * WCH)
            eng.wait_ge(s_xsp, 2)
            eng.wait_ge(t["s_ident"], 4)
            for s in range(SLOTS):
                if (j := at_slot(proj_slot, s)) is not None:
                    m0_free(0, j, 0, 0)
                    proj(0, j)
                if (j := at_slot(tp_slot, s)) is not None:
                    m1_free(0, j, 0, 0)
                    transposes(0, j)
            eng.wait_ge(s_ld["wo"], 16)
            heads(eng, slot)

        @block.scalar
        def _(eng):
            def read_proj(h, hb, j):
                J, G, g, b = 8 * h + j, 4 * h + j // 2, j // 2, j // 2 % 2
                r = 2 * (j % 2)
                wait(eng, s_pj, J + 1)
                if j % 2 == 0:
                    wait(eng, s_nrm, G - 3)
                    wait(eng, s_vl, G - 3)
                    wait(eng, s_ss, G - 1)
                m0 = M0[:, 0:2 * QKV].rearrange("p (r c) -> p r c", r=2)
                eng.activation(raw[:, g, r:r + 2, :], m0, ACT.Copy).then_inc(s_raw, 1)
                eng.activation(sq[:, b, r:r + 2, :, :], m0[:, :, 0:2 * DH].rearrange("p r (k d) -> p r k d", k=2),
                               ACT.Square).then_inc(s_sq, 1)

            def high_values(h, hb, g):
                wait(eng, s_raw, 8 * h + 2 * g + 2)
                wait(eng, s_av, SLOTS * (h - 1))
                eng.activation(V[:, hb, 4 * g:4 * g + 4, 0:DH], raw[:, g, :, 2 * DH:QKV], ACT.Copy).then_inc(s_vh, 1)

            def read_transposes(h, hb, j):
                wait(eng, s_tp, 8 * h + j + 1)
                eng.activation(QK[:, hb, :, 2 * P * j:2 * P * j + 2 * P],
                               M1[:, :].bitcast(F16)[:, 0:6 * P].rearrange("p (k c) -> p k c", k=3),
                               ACT.Copy).then_inc(s_tpa, 1)

            def read_out_transposes(i, u):
                wait(eng, s_ot, 8 * i + u + 1)
                eng.activation(OT[:, u, :, :], M1[:, 0:2 * P].rearrange("p (r c) -> p r c", r=2), ACT.Copy).then_inc(s_ote, 1)

            def read_out(i, s):
                b, u = s // SLOTS, s % SLOTS // 2
                m = 16 * i + 8 * b + u
                wait(eng, s_av, 2 * m + 2)
                wait(eng, s_o, m - 3)
                eng.activation(Or[:, u % 4, :], OP[u % 2][:, 0:258], ACT.Copy).then_inc(s_ob, 1)

            def exps(i, s):
                n, b = 32 * i + s, s // SLOTS
                if s % SLOTS == 0:
                    wait(eng, s_cur, 4 * i + 2 * b + 2)
                wait(eng, s_sc, n + 1)
                wait(eng, s_av, n - PB + 1)
                eng.activation(Pr[:, s % PB, :, :], SC[s % 2][:, :, :], ACT.Exp,
                               bias=cur_nesc[:, b:b + 1]).then_inc(s_ex, 1)

            def slot(i, s):
                h, sh = 2 * i + s // SLOTS, s % SLOTS
                if not ended(i):
                    exps(i, s)
                if (x := out_unit(s, turn_slot)) and exists(i, x[0]):
                    read_out_transposes(i - x[0], x[1])
                if s % 2 == 0:
                    if s >= 4 and not ended(i):
                        read_out(i, s - 4)
                    elif s < 4 and started(i, 1):
                        read_out(i - 1, s + 2 * SLOTS - 4)
                if prepares(i, s):
                    prepare(h + 1, (s // SLOTS + 1) % 2, sh)

            def prepare(h, hb, s):
                if (j := at_slot(proj_slot, s)) is not None:
                    read_proj(h, hb, j)
                if (g := at_slot(lambda g: GROUP_AT[g] + 2, s, 4)) is not None:
                    high_values(h, hb, g)
                if (j := at_slot(tp_slot, s)) is not None and j % 2:
                    read_transposes(h, hb, j)

            eng.wait_ge(s_ld["scl"], 16)
            eng.activation(esc[:, :], scl[:, :], ACT.Exp).then_inc(s_esc, 1)
            for s in range(SLOTS):
                prepare(0, 0, s)
            heads(eng, slot)

        @block.vector
        def _(eng):
            def square_sums(h, hb, g):
                G, b = 4 * h + g, g % 2
                wait(eng, s_sq, 8 * h + 2 * g + 2)
                eng.tensor_reduce(ss[:, b, :, :], sq[:, b, :, :, :], AX, ALU.add).then_inc(s_ss, 1)
                wait(eng, s_ss, G + 1)
                wait(eng, s_pw, G - 1)
                eng.tensor_scalar(ss2[:, b, :, :], ss[:, b, :, :], 1e-24, None, ALU.max).then_inc(s_cl, 1)

            def normalize(h, hb, g):
                G, b = 4 * h + g, g % 2
                wait(eng, s_rn, G + 1)
                wait(eng, s_raw, 8 * h + 2 * g + 2)
                wait(eng, s_hi, G - 1)
                wait(eng, s_lo, G - 1)
                qk = raw[:, g, :, 0:2 * DH].rearrange("p t (k d) -> p t k d", k=2)
                eng.tensor_tensor(nrm[:, b, :, :, :], qk, rn[:, b, :, :].unsqueeze(3).to_broadcast([P, 4, 2, DH]),
                                  ALU.mult).then_inc(s_nrm, 1)

            def high_parts(h, hb, g):
                G, b = 4 * h + g, g % 2
                wait(eng, s_nrm, G + 1)
                wait(eng, s_tp, 8 * (h - 1) + 2 * g + 2)
                out = stk[:, g, :, 0:4 * DH].rearrange("p t (k x) -> p t k x", k=2)[:, :, :, 0:DH]
                eng.tensor_copy(out, nrm[:, b, :, :, :]).then_inc(s_hi, 1)

            def copy_keys(h, hb, g):
                G, b = 4 * h + g, g % 2
                wait(eng, s_hi, G + 1)
                eng.tensor_copy(stk[:, g, :, 4 * DH:5 * DH], stk[:, g, :, 2 * DH:3 * DH]).then_inc(s_dup, 1)

            def read_transposes(h, hb, j):
                wait(eng, s_tp, 8 * h + j + 1)
                eng.tensor_copy(QK[:, hb, :, 2 * P * j:2 * P * j + 2 * P].bitcast(U32),
                                M1[:, 0:3 * P].bitcast(U32).rearrange("p (k c) -> p k c", k=3)).then_inc(s_tpd, 1)

            def low_probs(i, s):
                n = 32 * i + s
                wait(eng, s_ex, n + 1)
                wait(eng, s_av, n - PB + 1)
                pr = Pr[:, s % PB, :, :].rearrange("p a b -> p (a b)")
                eng.tensor_tensor(Pl[:, s % PB, :, :].rearrange("p a b -> p (a b)"), pr, high(pr)[:, 1::2],
                                  ALU.subtract).then_inc(s_pl, 1)

            def inverse_sums(i, s):
                b, u = s // SLOTS, s % SLOTS // 2
                m = 16 * i + 8 * b + u
                wait(eng, s_ob, m + 1)
                wait(eng, s_o, m - 3)
                eng.reciprocal(rden[:, u % 4, :], Or[:, u % 4, DH:DH + 130:129]).then_inc(s_dv, 1)

            def add_out(i, u):
                wait(eng, s_y, 8 * i + u + 1)
                acc = t["x"][:, 2 * u:2 * u + 2, :]
                eng.tensor_tensor(acc, acc, M0[:, 0:2 * P].rearrange("p (r c) -> p r c", r=2),
                                  ALU.add).then_inc(s_acc, 1)

            def head_scale(b, h):
                eng.tensor_copy(cur_esc[:, b:b + 1], esc[:, bass.ds(h, 1)]).then_inc(s_cur, 1)
                eng.tensor_scalar(cur_nesc[:, b:b + 1], esc[:, bass.ds(h, 1)], -1.0, None, ALU.mult).then_inc(s_cur, 1)

            def prepare(h, hb, s):
                if (j := at_slot(tp_slot, s)) is not None and j % 2 == 0:
                    read_transposes(h, hb, j)
                if s == 0:
                    head_scale(hb, h)
                if (g := at_slot(lambda g: GROUP_AT[g] + 2, s, 4)) is not None:
                    square_sums(h, hb, g)
                if (g := at_slot(lambda g: GROUP_AT[g] + 3, s, 4)) is not None:
                    normalize(h, hb, g)
                    high_parts(h, hb, g)
                    copy_keys(h, hb, g)

            def slot(i, s):
                h, sh = 2 * i + s // SLOTS, s % SLOTS
                if not ended(i) and sh not in POOL_LO:
                    low_probs(i, s)
                if (x := out_unit(s, out_slot)) and exists(i, x[0]):
                    add_out(i - x[0], x[1])
                if prepares(i, s):
                    prepare(h + 1, (s // SLOTS + 1) % 2, sh)
                if s % 2 == 0:
                    if s >= 4 and not ended(i):
                        inverse_sums(i, s - 4)
                    elif s < 4 and started(i, 1):
                        inverse_sums(i - 1, s + 2 * SLOTS - 4)


            eng.memset(V[:, :, :, DH:DH + 1], 1.0).then_inc(s_init, 1)
            eng.wait_ge(s_ld["xt"], 16)
            eng.tensor_copy(xT_hi[:, :], xT_f32).then_inc(s_xsp, 1)
            eng.wait_ge(s_xsp, 1)
            eng.tensor_tensor(xT_lo[:, :], xT_f32, xT_hi[:, :], ALU.subtract).then_inc(s_xsp, 1)
            eng.wait_ge(s_ld["w"], 16)
            for c in range(WCH):
                cs = slice(c * H * QKV // WCH, (c + 1) * H * QKV // WCH)
                eng.tensor_copy(w_hi[:, cs], w_f32[:, cs]).then_inc(s_wsp, 1)
                eng.wait_ge(s_wsp, 2 * c + 1)
                eng.tensor_tensor(w_lo[:, cs], w_f32[:, cs], w_hi[:, cs], ALU.subtract).then_inc(s_wsp, 1)
            eng.wait_ge(s_ld["x"], 32)
            eng.tensor_tensor(t["x"][:, :, :], t["x"][:, :, :],
                              t["bout"][:, :].unsqueeze(1).to_broadcast([P, NT, D]), ALU.add).then_inc(s_xb, 1)
            eng.wait_ge(s_esc, 1)
            for s in range(SLOTS):
                prepare(0, 0, s)
            eng.wait_ge(s_xb, 1)
            heads(eng, slot)

        @block.gpsimd
        def _(eng):
            def low_probs(i, s):
                n = 32 * i + s
                wait(eng, s_ex, n + 1)
                wait(eng, s_av, n - PB + 1)
                pr = Pr[:, s % PB, :, :].rearrange("p a b -> p (a b)")
                eng.tensor_tensor(Pl[:, s % PB, :, :].rearrange("p a b -> p (a b)"), pr, high(pr)[:, 1::2],
                                  ALU.subtract).then_inc(s_plp, 1)

            def divide(i, s):
                b, u = s // SLOTS, s % SLOTS // 2
                m = 16 * i + 8 * b + u
                wait(eng, s_ob, m + 1)
                o = Or[:, u % 4, :].rearrange("p (r c) -> p r c", r=2)
                eng.tensor_tensor(osum[:, u % 2, :, :], o[:, :, 0:DH], o[:, :, DH + 1:], ALU.add).then_inc(s_os, 1)
                wait(eng, s_os, m + 1)
                wait(eng, s_dv, m + 1)
                eng.tensor_tensor(Ob[:, 2 * u:2 * u + 2, DH * b:DH * b + DH], osum[:, u % 2, :, :],
                                  rden[:, u % 4, :].unsqueeze(2).to_broadcast([P, 2, DH]), ALU.mult).then_inc(s_o, 1)

            def inverse_norms(h, hb, g):
                G, b = 4 * h + g, g % 2
                wait(eng, s_cl, G + 1)
                wait(eng, s_nrm, G - 1)
                eng.tensor_tensor(rn[:, b, :, :], ss2[:, b, :, :],
                                  half[:, 0:1].unsqueeze(2).to_broadcast([P, 4, 2]), ALU.pow).then_inc(s_pw, 1)
                wait(eng, s_pw, G + 1)
                wait(eng, s_cur, 2 * h + 1)
                eng.tensor_tensor(rn[:, b, :, 0], rn[:, b, :, 0],
                                  cur_esc[:, hb:hb + 1].to_broadcast([P, 4]), ALU.mult).then_inc(s_rn, 1)

            def low_values(h, hb, g):
                G, b = 4 * h + g, g % 2
                wait(eng, s_raw, 8 * h + 2 * g + 2)
                wait(eng, s_vh, G + 1)
                v = V[:, hb, 4 * g:4 * g + 4, :]
                eng.tensor_tensor(v[:, :, DH + 1:2 * DH + 1], raw[:, g, :, 2 * DH:QKV], v[:, :, 0:DH],
                                  ALU.subtract).then_inc(s_vl, 1)

            def low_parts(h, hb, g):
                G, b = 4 * h + g, g % 2
                wait(eng, s_hi, G + 1)
                both = stk[:, g, :, 0:4 * DH].rearrange("p t (k x) -> p t k x", k=2)
                eng.tensor_tensor(both[:, :, :, DH:2 * DH], nrm[:, b, :, :, :], both[:, :, :, 0:DH],
                                  ALU.subtract).then_inc(s_lo, 1)

            def prepare(h, hb, s):
                if (g := at_slot(lambda g: GROUP_AT[g] + 2, s, 4)) is not None:
                    inverse_norms(h, hb, g)
                    low_values(h, hb, g)
                if (g := at_slot(lambda g: GROUP_AT[g] + 3, s, 4)) is not None:
                    low_parts(h, hb, g)

            def slot(i, s):
                h, sh = 2 * i + s // SLOTS, s % SLOTS
                if not ended(i) and sh in POOL_LO:
                    low_probs(i, s)
                if prepares(i, s):
                    prepare(h + 1, (s // SLOTS + 1) % 2, sh)
                if s % 2 == 0:
                    if s >= 4 and not ended(i):
                        divide(i, s - 4)
                    elif s < 4 and started(i, 1):
                        divide(i - 1, s + 2 * SLOTS - 4)

            for m in (t["ident16"], t["ident32"]):
                eng.memset(m[:, :], 0.0).then_inc(t["s_ident"], 1)
            eng.memset(half[:, :], -0.5).then_inc(s_half, 1)
            eng.wait_ge(t["s_ident"], 2)
            for m in (t["ident16"], t["ident32"]):
                eng.affine_select(out=m[:, :], in_=m[:, :], compare_op=ALU.not_equal, fill=1.0, base=0,
                                  pattern=[[-1, P]], channel_multiplier=1).then_inc(t["s_ident"], 1)
            eng.wait_ge(s_half, 1)
            for s in range(SLOTS):
                prepare(0, 0, s)
            heads(eng, slot)

    sem.end()


TB = NT // B
G2 = 2
TG = S // G2


def normalize_and_turn(nc, tag, t, io, batches, adds, route, stores):
    es = ExitStack()
    sem = Semaphores(nc, tag)
    with es:
        def sb(name, shape, dt):
            return es.enter_context(nc.sbuf_tensor(f"{name}_{tag}", shape, dt))

        x, xT, xl = t["x"], t["xT"], t["xl"]
        stats = sb("stats", [P, B, TB, 6], F32)
        mv = sb("mv", [P, B, TB, 2], F32)
        ve = sb("ve", [P, B, TB], F32)
        rstd = sb("rstd", [P, B, TB], F32)
        lg = sb("lg", [P, B, TB, E], F32)
        mx = sb("mx", [P, B, TB, 8], F32)
        ix = sb("ix", [P, B, TB, 8], U32)
        ixf = sb("ixf", [P, B, TB, 2], F32)
        df = sb("df", [P, B, TB], F32)
        ex = sb("ex", [P, B, TB], F32)
        e1 = sb("e1", [P, B, TB], F32)
        p1 = sb("p1", [P, B, TB], F32)
        p2 = sb("p2", [P, B, TB], F32)
        m1 = sb("m1", [P, B, TB, E], F32)
        m2 = sb("m2", [P, B, TB, E], F32)
        TP = [es.enter_context(nc.psum_tensor(f"TP{i}_{tag}", [P, 4, P], F32)) for i in range(4)]
        LG = [es.enter_context(nc.psum_tensor(f"LG{i}_{tag}", [P, TB, E], F32)) for i in range(2)]

        s_yt, s_add, s_st, s_mv, s_ve, s_rs, s_xn, s_tp, s_xt, s_xl, s_out = (
            sem(n) for n in ("g_yt", "g_add", "g_st", "g_mv", "g_ve", "g_rs", "g_xn", "g_tp", "g_xt", "g_xl", "g_out"))
        s_lg, s_lc, s_mx, s_ix, s_df, s_ex, s_e1, s_p1, s_p2, s_eq, s_ml, s_cw = (
            sem(n) for n in ("g_lg", "g_lc", "g_mx", "g_ix", "g_df", "g_ex", "g_e1", "g_p1", "g_p2", "g_eq",
                             "g_ml", "g_cw"))
        block = es.enter_context(nc.Block())
        n_of = {b: n for n, b in enumerate(batches)}

        @block.sync
        def _(eng):
            if stores:
                for b in batches:
                    eng.wait_ge(s_xn, TB * (n_of[b] + 1))
                    eng.dma_start(stores[b].rearrange("(t p) d -> p t d", p=P),
                                  x[:, TB * b:TB * b + TB, :]).then_inc(s_out, 16)
                eng.wait_ge(s_out, 16 * len(batches))

        @block.tensor
        def _(eng):
            for b in batches:
                n = n_of[b]
                if adds:
                    for k in range(2):
                        wait(eng, s_xt, 2 * (n - 1) + k + 1)
                        for r in range(4):
                            mm = eng.transpose(TP[k][:, r, :], t[adds][:, b, (4 * k + r) * P:(4 * k + r + 1) * P],
                                               t["ident32"][:, :])
                        mm.then_inc(s_yt, 1)
                if stores:
                    continue
                for k in range(2):
                    bank = TP[2 + k] if adds else TP[2 * n + k]
                    eng.wait_ge(s_xn, TB * n + 4 * k + 4)
                    if adds:
                        wait(eng, s_xt, 2 * (n - 1) + k + 1)
                    for r in range(4):
                        mm = eng.transpose(bank[:, r, :], x[:, TB * b + 4 * k + r, :], t["ident32"][:, :])
                    mm.then_inc(s_tp, 1)
                if route:
                    for k in range(TB):
                        if k % 4 == 0:
                            eng.wait_ge(s_xt, 2 * n + k // 4 + 1)
                        col = b * S + k * P
                        mm = eng.matmul(LG[n][:, k, :], xT[:, col:col + P], t[route][:, :], start=True, stop=True)
                    mm.then_inc(s_lg, 1)

        @block.scalar
        def _(eng):
            if stores:
                return
            for b in batches:
                n = n_of[b]
                for k in range(2):
                    bank = TP[2 + k] if adds else TP[2 * n + k]
                    eng.wait_ge(s_tp, 2 * n + k + 1)
                    col = b * S + 4 * k * P
                    eng.activation(xT[:, col:col + 4 * P], bank[:, :, :].rearrange("p r c -> p (r c)"),
                                   ACT.Copy).then_inc(s_xt, 1)
            if route:
                for b in batches:
                    n = n_of[b]
                    eng.wait_ge(s_df, n + 1)
                    eng.activation(ex[:, b, :], df[:, b, :], ACT.Exp).then_inc(s_ex, 1)

        @block.gpsimd
        def _(eng):
            for b in batches:
                n = n_of[b]
                eng.wait_ge(s_ve, n + 1)
                eng.tensor_tensor(rstd[:, b, :], ve[:, b, :], t["half"][:, 0:1].to_broadcast([P, TB]),
                                  ALU.pow).then_inc(s_rs, 1)

        @block.vector
        def _(eng):
            def statistics(b):
                n = n_of[b]
                if adds:
                    for k in range(2):
                        eng.wait_ge(s_yt, 2 * n + k + 1)
                        xs = x[:, TB * b + 4 * k:TB * b + 4 * k + 4, :]
                        eng.tensor_tensor(xs, xs, TP[k][:, :, :], ALU.add).then_inc(s_add, 1)
                    eng.wait_ge(s_add, 2 * n + 2)
                for k in range(TB):
                    eng.bn_stats(stats[:, b, k, :], x[:, TB * b + k, :]).then_inc(s_st, 1)
                for k in range(TB):
                    eng.wait_ge(s_st, TB * n + k + 1)
                    eng.bn_aggr(mv[:, b, k, :], stats[:, b, k, :]).then_inc(s_mv, 1)
                eng.wait_ge(s_mv, TB * (n + 1))
                eng.tensor_scalar(ve[:, b, :], mv[:, b, :, 1], EPS, None, ALU.add).then_inc(s_ve, 1)

            def rows(b):
                n = n_of[b]
                eng.wait_ge(s_rs, n + 1)
                for k in range(TB):
                    xs = x[:, TB * b + k, :]
                    eng.tensor_scalar(xs, xs, mv[:, b, k, 0:1], rstd[:, b, k:k + 1], ALU.subtract,
                                      ALU.mult).then_inc(s_xn, 1)

            def low(b):
                n = n_of[b]
                for k in range(2):
                    eng.wait_ge(s_xt, 2 * n + k + 1)
                    xs = xT[:, b * S + 4 * k * P:b * S + 4 * (k + 1) * P]
                    eng.tensor_tensor(xl[:, b * S + 4 * k * P:b * S + 4 * (k + 1) * P], xs, high(xs)[:, 1::2],
                                      ALU.subtract).then_inc(s_xl, 1)

            def choose(b):
                n = n_of[b]
                eng.wait_ge(s_lg, n + 1)
                eng.tensor_copy(lg[:, b, :, :], LG[n][:, :, :]).then_inc(s_lc, 1)
                eng.wait_ge(s_lc, n + 1)
                for k in range(TB):
                    eng.max(mx[:, b, k, :], lg[:, b, k, :]).then_inc(s_mx, 1)
                eng.wait_ge(s_mx, TB * (n + 1))
                eng.tensor_tensor(df[:, b, :], mx[:, b, :, 1], mx[:, b, :, 0], ALU.subtract).then_inc(s_df, 1)
                for k in range(TB):
                    eng.max_index(ix[:, b, k, :], mx[:, b, k, :], lg[:, b, k, :]).then_inc(s_ix, 1)
                eng.wait_ge(s_ix, (TB + 1) * n + TB)
                eng.tensor_copy(ixf[:, b, :, :], ix[:, b, :, 0:2]).then_inc(s_ix, 1)

            def combine(b):
                n = n_of[b]
                eng.wait_ge(s_ex, n + 1)
                eng.tensor_scalar(e1[:, b, :], ex[:, b, :], 1.0, None, ALU.add).then_inc(s_e1, 1)
                eng.wait_ge(s_e1, n + 1)
                eng.reciprocal(p1[:, b, :], e1[:, b, :]).then_inc(s_p1, 1)
                iota = t["iota"][:, :].unsqueeze(1).to_broadcast([P, TB, E])
                for k, m in enumerate((m1, m2)):
                    eng.tensor_tensor(m[:, b, :, :], iota, ixf[:, b, :, k:k + 1].to_broadcast([P, TB, E]),
                                      ALU.is_equal).then_inc(s_eq, 1)
                eng.wait_ge(s_p1, n + 1)
                eng.tensor_tensor(p2[:, b, :], ex[:, b, :], p1[:, b, :], ALU.mult).then_inc(s_p2, 1)
                eng.wait_ge(s_p2, n + 1)
                eng.wait_ge(s_eq, 2 * n + 2)
                for m, pr in ((m1, p1), (m2, p2)):
                    eng.tensor_tensor(m[:, b, :, :], m[:, b, :, :],
                                      pr[:, b, :].unsqueeze(2).to_broadcast([P, TB, E]), ALU.mult).then_inc(s_ml, 1)
                eng.wait_ge(s_ml, 2 * n + 2)
                eng.tensor_tensor(t["cw"][:, TB * b:TB * b + TB, 0:E], m1[:, b, :, :], m2[:, b, :, :],
                                  ALU.add).then_inc(s_cw, 1)

            for b in batches:
                statistics(b)
                rows(b)
            if stores:
                return
            for b in batches:
                low(b)
                if route:
                    choose(b)
            if route:
                for b in batches:
                    n = n_of[b]
                    eng.wait_ge(s_ix, (TB + 1) * (n + 1))
                    combine(b)

    sem.end()


def prepare_rest(nc, t, io):
    es = ExitStack()
    sem = Semaphores(nc, "pr")
    with es:
        def sb(name, shape, dt):
            return es.enter_context(nc.sbuf_tensor(name, shape, dt))

        al, ab, na, en, ln, mxa = (sb("c_" + n, [P, 16], F32) for n in ("al", "ab", "na", "en", "ln", "mxa"))
        bb, cc = sb("c_b", [P, 16], F32), sb("c_c", [P, 16], F32)
        io_i = sb("io_i", [P, E], mybir.dt.int32)
        s_d, s_i, s_v, s_a = sem("c_d"), sem("c_i"), sem("c_v"), sem("c_a")
        block = es.enter_context(nc.Block())

        @block.sync
        def _(eng):
            for dst, name in ((al[:, :], "a_log"), (bb[:, :], "b"), (cc[:, :], "c"), (t["dtw"][:, :], "dtwT"),
                              (t["dtb"][:, :], "dt_b"), (t["cvw"][:, :], "conv_w"), (t["cvb"][:, :], "conv_b"),
                              (t["gate"][:, :], "gateT"), (t["router"][:, :], "routerT")):
                eng.dma_start(dst, io[name]).then_inc(s_d, 16)
            eng.wait_ge(s_d, 16 * 9)

        @block.gpsimd
        def _(eng):
            eng.iota(io_i[:, :], pattern=[[1, E]], base=0, channel_multiplier=0).then_inc(s_i, 1)
            eng.memset(t["half"][:, :], -0.5).then_inc(s_i, 1)
            eng.memset(t["cw"][:, :, E:E + 1], 1.0).then_inc(s_i, 1)
            eng.wait_ge(s_i, 3)
            eng.tensor_copy(t["iota"][:, :], io_i[:, :]).then_inc(s_i, 1)

        @block.vector
        def _(eng):
            eng.wait_ge(s_d, 16 * 9)
            eng.tensor_scalar(na[:, :], al[:, :], -1.0, None, ALU.mult).then_inc(s_v, 1)
            eng.tensor_tensor(t["bc"][:, :], bb[:, :], cc[:, :], ALU.mult).then_inc(s_v, 1)
            eng.tensor_scalar(mxa[:, :], al[:, :], 0.0, None, ALU.max).then_inc(s_v, 1)
            eng.wait_ge(s_v, 3)
            eng.tensor_tensor(ab[:, :], al[:, :], na[:, :], ALU.min).then_inc(s_v, 1)
            eng.wait_ge(s_a, 2)
            eng.tensor_tensor(na[:, :], mxa[:, :], ln[:, :], ALU.add).then_inc(s_v, 1)
            eng.wait_ge(s_v, 5)
            eng.tensor_scalar(t["A"][:, :], na[:, :], -1.0, None, ALU.mult).then_inc(s_v, 1)

        @block.scalar
        def _(eng):
            eng.wait_ge(s_v, 4)
            eng.activation(en[:, :], ab[:, :], ACT.Exp).then_inc(s_a, 1)
            eng.wait_ge(s_a, 1)
            eng.activation(ln[:, :], en[:, :], ACT.Ln, bias=1.0).then_inc(s_a, 1)

    sem.end()


DS = 16


def experts(nc, tag, t, io, layer, b, ssm):
    NE = E + layer
    W = (3, 2)[layer] * FF
    DOWN = (2, 1)[layer] * FF
    es = ExitStack()
    sem = Semaphores(nc, tag)
    with es:
        def sb(name, shape, dt):
            return es.enter_context(nc.sbuf_tensor(f"{name}_{tag}", shape, dt))

        x, xT, xl, cw = t["x"], t["xT"], t["xl"], t["cw"]
        wf = sb("wf", [P, 2, W], F32)
        wh = sb("wh", [P, 2, W], F16)
        wl = sb("wl", [P, 2, W], F16)
        act = sb("act", [P, 2, TG], F32)
        hid = sb("hid", [P, 2, NC, TG], F32)
        hlo = sb("hlo", [P, 2, NC, TG], F16)
        GB = [es.enter_context(nc.psum_tensor(f"GB{i}_{tag}", [P, TG], F32)) for i in range(2)]
        UB = [es.enter_context(nc.psum_tensor(f"UB{i}_{tag}", [P, TG], F32)) for i in range(2)]
        DB = [es.enter_context(nc.psum_tensor(f"DB{i}_{tag}", [P, 4, P], F32)) for i in range(2)]
        DT = [es.enter_context(nc.psum_tensor(f"DT{i}_{tag}", [P, TG], F32)) for i in range(2)]
        if ssm is not None:
            xf = sb("xf", [P, S], F32)
            sg = sb("sg", [P, S], F32)
            dt = sb("dt", [P, S], F32)
            us = sb("us", [P, S], F32)
            ea = sb("ea", [P, 2, S], F32)
            bu = sb("bu", [P, 2, S], F32)
            st = sb("st", [P, 2, S], F32)

        s_w = [sem(f"w{i}") for i in range(2)]
        (s_wh, s_wl, s_gu, s_act, s_hid, s_hp, s_lo, s_dn, s_ac, s_xf, s_dtp, s_sg, s_dt, s_us, s_ea, s_bu, s_st,
         s_y) = (sem(n) for n in ("wh", "wl", "gu", "act", "hid", "hp", "lo", "dn", "ac", "xf", "dtp", "sg", "dt",
                                  "us", "ea", "bu", "st", "y"))
        block = es.enter_context(nc.Block())
        w_io = io[f"w{layer}"]

        def each(eng, emit, end=None):
            for k in range(2):
                emit(0, k)
            with eng.Fori(1, (NE - 1) // 2) as i:
                for k in range(2):
                    emit(i, k)
            for e in range(2 * ((NE - 1) // 2), NE):
                emit(e // 2, e % 2)
            if end:
                end()

        def with_ssm(i):
            return ssm is not None and not (isinstance(i, int) and i == E // 2)

        @block.sync
        def _(eng):
            def load(i, k):
                wait(eng, s_wh, 2 * i + k - 1)
                wait(eng, s_wl, 2 * i + k - 1)
                eng.dma_start(wf[:, k, :], w_io[:, bass.ds(W * (2 * i + k), W)]).then_inc(s_w[k], 16)

            each(eng, load)

        @block.tensor
        def _(eng):
            def unit(i, k, g, c):
                U = 16 * i + 8 * k + 4 * g + c
                e = 2 * i + k
                if g == 0 and c == 0:
                    wait(eng, s_wh, e + 1)
                    wait(eng, s_wl, e + 1)
                wait(eng, s_act, U - 1)
                if layer == 0:
                    wait(eng, s_hid, U - 1)
                col = b * S + g * TG
                xh, xlo = high(xT[:, col:col + TG])[:, 1::2], xl[:, col:col + TG]
                for m, bank in enumerate((GB, UB)[:2 - layer]):
                    at = m * FF + P * c
                    eng.matmul(bank[c % 2][:, :], wh[:, k, at:at + P], xh, start=True, stop=False)
                    eng.matmul(bank[c % 2][:, :], wl[:, k, at:at + P], xh, start=False, stop=False)
                    mm = eng.matmul(bank[c % 2][:, :], wh[:, k, at:at + P], xlo, start=False, stop=True)
                mm.then_inc(s_gu, 1)

            def down(i, k, g, tile):
                Q = 4 * i + 2 * k + g
                if tile == 0:
                    wait(eng, s_lo, 4 * Q + 4)
                    wait(eng, s_ac, 4 * (Q - 1))
                for c in range(NC):
                    h = high(hid[:, g, c, P * tile:P * tile + P])[:, 1::2]
                    hl = hlo[:, g, c, P * tile:P * tile + P]
                    at = DOWN + P * c
                    out = DB[g][:, tile, :]
                    eng.matmul(out, h, wh[:, k, at:at + P], start=c == 0, stop=False)
                    eng.matmul(out, h, wl[:, k, at:at + P], start=False, stop=False)
                    mm = eng.matmul(out, hl, wh[:, k, at:at + P], start=False, stop=c == NC - 1)
                if tile == 3:
                    mm.then_inc(s_dn, 1)

            def before(i, k, g):
                if g:
                    return i, k, 0
                if k:
                    return i, 0, 1
                return None if isinstance(i, int) and i == 0 else (i - 1, 1, 1)

            def expert(i, k):
                for g in range(2):
                    for c in range(NC):
                        unit(i, k, g, c)
                        if q := before(i, k, g):
                            for tile in ((), (0,), (1, 2), (3,))[c]:
                                down(*q, tile)

            def end():
                for tile in range(4):
                    down(*((E // 2 - 1, 1, 1) if NE == E else (E // 2, 0, 1)), tile)

            if ssm is not None:
                for m in range(2):
                    eng.wait_ge(s_xf, 3)
                    eng.matmul(DT[m][:, :], t["dtw"][:, :], xf[:, m * TG:m * TG + TG], start=True,
                               stop=True).then_inc(s_dtp, 1)
            each(eng, expert, end)

        @block.scalar
        def _(eng):
            def unit(i, k, g, c):
                U = 16 * i + 8 * k + 4 * g + c
                Q = 4 * i + 2 * k + g
                wait(eng, s_gu, U + 1)
                if layer == 0:
                    wait(eng, s_hid, U - 1)
                    eng.activation(act[:, c % 2, :], GB[c % 2][:, :], ACT.Silu).then_inc(s_act, 1)
                else:
                    wait(eng, s_hp, 8 * i + 4 * k + 2 * g + c // 2)
                    wait(eng, s_hid, 8 * i + 4 * k + 2 * g + c // 2)
                    eng.activation(act[:, c % 2, :], GB[c % 2][:, :], ACT.Relu).then_inc(s_act, 1)
                    if c % 2 == 0:
                        wait(eng, s_act, U + 1)
                        if c == 0:
                            wait(eng, s_dn, Q - 1)
                        eng.activation(hid[:, g, c, :], act[:, c % 2, :], ACT.Square).then_inc(s_hid, 1)

            def state(i, d):
                n = 4 * i + d
                wait(eng, s_st, n - 1)
                eng.activation(ea[:, d % 2, :], dt[:, :], ACT.Exp, scale=t["A"][:, bass.ds(n, 1)]).then_inc(s_ea, 1)
                eng.activation(bu[:, d % 2, :], us[:, :], ACT.Copy, scale=t["bc"][:, bass.ds(n, 1)]).then_inc(s_bu, 1)

            def expert(i, k):
                for g in range(2):
                    for c in range(NC):
                        unit(i, k, g, c)
                    if with_ssm(i):
                        state(i, 2 * k + g)

            if ssm is not None:
                for m in range(2):
                    eng.wait_ge(s_dtp, m + 1)
                    eng.activation(sg[:, m * TG:m * TG + TG], DT[m][:, :], ACT.Sigmoid,
                                   bias=t["dtb"][:, 0:1]).then_inc(s_sg, 1)
                eng.wait_ge(s_us, 1)
            each(eng, expert)

        @block.vector
        def _(eng):
            def split(i, k):
                e = 2 * i + k
                wait(eng, s_w[k], 16 * (i + 1))
                wait(eng, s_dn, 2 * (e - 1))
                eng.tensor_copy(wh[:, k, :], wf[:, k, :]).then_inc(s_wh, 1)

            def unit(i, k, g, c):
                U = 16 * i + 8 * k + 4 * g + c
                Q = 4 * i + 2 * k + g
                h = hid[:, g, c, :]
                if layer == 0:
                    wait(eng, s_act, U + 1)
                    if c == 0:
                        wait(eng, s_dn, Q - 1)
                    eng.tensor_tensor(h, act[:, c % 2, :], UB[c % 2][:, :], ALU.mult).then_inc(s_hid, 1)
                    wait(eng, s_hid, U + 1)
                else:
                    wait(eng, s_hp if c % 2 else s_hid, 8 * i + 4 * k + 2 * g + c // 2 + 1)
                eng.tensor_tensor(hlo[:, g, c, :], h, high(h)[:, 1::2], ALU.subtract).then_inc(s_lo, 1)

            def add(i, k, g):
                Q = 4 * i + 2 * k + g
                e = 2 * i + k
                wait(eng, s_dn, Q + 1)
                for tile in range(4):
                    xs = x[:, TB * b + 4 * g + tile, :]
                    eng.scalar_tensor_tensor(out=xs, in0=DB[g][:, tile, :],
                                             scalar=cw[:, TB * b + 4 * g + tile, bass.ds(e, 1)], in1=xs,
                                             op0=ALU.mult, op1=ALU.add).then_inc(s_ac, 1)

            def scan(i, d):
                n = 4 * i + d
                wait(eng, s_bu, n + 1)
                wait(eng, s_ea, n + 1)
                wait(eng, s_y, n - 1)
                eng.tensor_tensor_scan(st[:, d % 2, :], ea[:, d % 2, :], bu[:, d % 2, :], 0.0, ALU.mult,
                                       ALU.add).then_inc(s_st, 1)

            def expert(i, k):
                for g in range(2):
                    for c in range(NC):
                        unit(i, k, g, c)
                        if c == 0 and g == 1:
                            if k == 0 and not (isinstance(i, int) and 2 * i + 1 >= NE):
                                split(i, 1)
                            elif k == 1 and not (isinstance(i, int) and 2 * i + 2 >= NE):
                                split(i + 1, 0)
                        if c == 1 and (q := expert_before(i, k, g)):
                            add(*q)
                    if with_ssm(i):
                        scan(i, 2 * k + g)

            def expert_before(i, k, g):
                if k:
                    return i, 0, g
                return None if isinstance(i, int) and i == 0 else (i - 1, 1, g)

            if ssm is not None:
                xs = xT[:, ssm * S:ssm * S + S]
                eng.tensor_scalar(xf[:, :], xs, t["cvw"][:, 1:2], t["cvb"][:, 0:1], ALU.mult, ALU.add).then_inc(s_xf, 1)
                eng.wait_ge(s_xf, 1)
                eng.scalar_tensor_tensor(out=xf[:, 1:S], in0=xs[:, 0:S - 1], scalar=t["cvw"][:, 0:1], in1=xf[:, 1:S],
                                         op0=ALU.mult, op1=ALU.add).then_inc(s_xf, 1)
                eng.wait_ge(s_xf, 2)
                eng.scalar_tensor_tensor(out=xf[:, 0:S - 1], in0=xs[:, 1:S], scalar=t["cvw"][:, 2:3],
                                         in1=xf[:, 0:S - 1], op0=ALU.mult, op1=ALU.add).then_inc(s_xf, 1)
                split(0, 0)
                eng.wait_ge(s_sg, 2)
                eng.tensor_scalar(dt[:, :], sg[:, :], 0.1 - 0.001, 0.001, ALU.mult, ALU.add).then_inc(s_dt, 1)
                eng.wait_ge(s_dt, 1)
                eng.tensor_tensor(us[:, :], dt[:, :], xf[:, :], ALU.mult).then_inc(s_us, 1)
            else:
                split(0, 0)

            def last():
                for g in range(2):
                    add(*((E // 2 - 1, 1, g) if NE == E else (E // 2, 0, g)))

            each(eng, expert, last)

        @block.gpsimd
        def _(eng):
            def split(i, k):
                e = 2 * i + k
                wait(eng, s_wh, e + 1)
                eng.tensor_tensor(wl[:, k, :], wf[:, k, :], wh[:, k, :], ALU.subtract).then_inc(s_wl, 1)

            def square(i, k, g, c):
                U = 16 * i + 8 * k + 4 * g + c
                Q = 4 * i + 2 * k + g
                wait(eng, s_act, U + 1)
                if c == 1:
                    wait(eng, s_dn, Q - 1)
                eng.tensor_tensor(hid[:, g, c, :], act[:, c % 2, :], act[:, c % 2, :], ALU.mult).then_inc(s_hp, 1)

            def sum_state(i, d):
                n = 4 * i + d
                wait(eng, s_st, n + 1)
                y = t["y"][:, ssm, :]
                if d == 0 and isinstance(i, int) and i == 0:
                    eng.tensor_copy(y, st[:, 0, :]).then_inc(s_y, 1)
                else:
                    wait(eng, s_y, n)
                    eng.tensor_tensor(y, y, st[:, d % 2, :], ALU.add).then_inc(s_y, 1)

            def expert(i, k):
                for g in range(2):
                    for c in range(NC):
                        if layer and c % 2:
                            square(i, k, g, c)
                        if g == 1 and c == 0:
                            if k == 0 and not (isinstance(i, int) and 2 * i + 1 >= NE):
                                split(i, 1)
                            elif k == 1 and not (isinstance(i, int) and 2 * i + 2 >= NE):
                                split(i + 1, 0)
                    if with_ssm(i):
                        sum_state(i, 2 * k + g)

            split(0, 0)
            each(eng, expert)

    sem.end()


def program(nc, io, out):
    ctx = ExitStack()
    with ctx:
        def sb(name, shape, dt):
            return ctx.enter_context(nc.sbuf_tensor(name, shape, dt))

        t = {
            "x": sb("x", [P, NT, D], F32),
            "ident16": sb("ident16", [P, P], F16),
            "ident32": sb("ident32", [P, P], F32),
            "s_ident": ctx.enter_context(nc.semaphore("s_ident")),
        }
        with nc.sbuf_tensor("bout", [P, D], F32) as bout:
            attention(nc, ctx, io, t | {"bout": bout})
        t |= {
            "xT": sb("xT", [P, T], F32),
            "xl": sb("xl", [P, T], F16),
            "y": sb("y", [P, B, S], F32),
            "cw": sb("cw", [P, NT, E + 1], F32),
            "iota": sb("iota", [P, E], F32),
            "half": sb("half", [P, 1], F32),
            "gate": sb("gate", [P, E], F32),
            "router": sb("router", [P, E], F32),
            "dtw": sb("dtw", [P, D], F32),
            "dtb": sb("dtb", [P, 1], F32),
            "cvw": sb("cvw", [P, 3], F32),
            "cvb": sb("cvb", [P, 1], F32),
            "A": sb("A", [P, DS], F32),
            "bc": sb("bc", [P, DS], F32),
        }
        prepare_rest(nc, t, io)
        normalize_and_turn(nc, "n1", t, io, (0, 1), None, "gate", None)
        experts(nc, "e2", t, io, 0, 0, None)
        normalize_and_turn(nc, "n3", t, io, (0,), None, None, None)
        experts(nc, "e4", t, io, 0, 1, 0)
        normalize_and_turn(nc, "n5", t, io, (0,), "y", "router", None)
        normalize_and_turn(nc, "n6", t, io, (1,), None, None, None)
        experts(nc, "e7", t, io, 1, 0, 1)
        normalize_and_turn(nc, "n8", t, io, (1,), "y", "router", None)
        normalize_and_turn(nc, "n9", t, io, (0,), None, None, {0: out[0]})
        experts(nc, "e10", t, io, 1, 1, None)
        normalize_and_turn(nc, "n11", t, io, (1,), None, None, {1: out[1]})


def layout(inputs):
    import numpy as np
    a = {k: np.asarray(v) for k, v in inputs.items()}
    x = a["L0_attn_x"].reshape(T, D)
    wq = a["L0_attn_w_q"].reshape(D, H, DH)
    wkv = a["L0_attn_w_kv"].reshape(D, 2, H, DH)

    def up(w):
        return w.transpose(2, 0, 1)

    def down(w):
        return w.reshape(-1, D, NC, P).transpose(3, 0, 2, 1).reshape(P, -1, NC * D)

    w_fc = np.concatenate([a["L1_ffn_w_fc"], a["L1_ffn_shared_fc"][None]])
    w_proj = np.concatenate([a["L1_ffn_w_proj"], a["L1_ffn_shared_proj"][None]])
    named = {
        "x": x,
        "xT": x.T,
        "wqkv": np.concatenate([wq, wkv[:, 0], wkv[:, 1]], axis=2).reshape(D, H * QKV),
        "wout": a["L0_attn_w_out"].reshape(H // 2, P, D).transpose(1, 0, 2).reshape(P, H // 2 * D),
        "b_out": a["L0_attn_b_out"],
        "scale": a["L0_attn_scale"].reshape(H),
        "w0": np.concatenate([up(a["L0_ffn_wg"]), up(a["L0_ffn_wu"]), down(a["L0_ffn_wd"])], axis=2).reshape(P, -1),
        "w1": np.concatenate([up(w_fc), down(w_proj)], axis=2).reshape(P, -1),
        "gateT": a["L0_ffn_gate_w"].T,
        "routerT": a["L1_ffn_router_w"].T,
        "a_log": a["L1_attn_a_log"],
        "b": a["L1_attn_b"],
        "c": a["L1_attn_c"],
        "dtwT": a["L1_attn_dt_w"].T,
        "dt_b": a["L1_attn_dt_b"].reshape(D, 1),
        "conv_w": a["L1_attn_conv_w"].reshape(D, 3),
        "conv_b": a["L1_attn_conv_b"].reshape(D, 1),
    }
    return {k: np.ascontiguousarray(v) for k, v in named.items()}


def kernel(**inputs):
    import numpy as np
    import concourse.bacc as bacc
    from concourse.bass_utils import run_bass_kernel_spmd as run

    nc = bacc.Bacc("TRN2", target_bir_lowering=False, num_devices=1)
    arrays = {f"in_{k}": v for k, v in layout(inputs).items()}
    io = {k[3:]: nc.dram_tensor(k, a.shape, mybir.dt.from_np(a.dtype), kind="ExternalInput").ap()
          for k, a in arrays.items()}
    out = nc.dram_tensor("out", (B, S, D), F32, kind="ExternalOutput").ap()
    program(nc, io, out)
    return run(nc, [arrays], core_ids=[0]).results[0]["out"]
```

```python
import concourse.bass as bass
from concourse import mybir
from contextlib import ExitStack

F32 = mybir.dt.float32
F16 = mybir.dt.float16
BF16 = mybir.dt.bfloat16
U32 = mybir.dt.uint32
ALU = mybir.AluOpType
ACT = mybir.ActivationFunctionType
AX = mybir.AxisListType.X

P = 128
B, S, D = 2, 1024, 128
T = B * S
NT = T // P
H, DH = 16, 64
QKV = 3 * DH
E = 8
FF = 512
NC = FF // P
EPS = 1e-5


def high(ap):
    return ap.bitcast(BF16)


def wait(eng, sem, count):
    if not isinstance(count, int) or count > 0:
        eng.wait_ge(sem, count)


SLOTS = 16
QW = 256
KT = 4
PB = 4
LAG = 2
PJ = 8
VW = 130
STK = 5 * DH
WCH = 4


TAIL = 32
POOL_LO = (4, 13, 15)
GROUP_AT = (0, 3, 6, 8)


def low_count(i, s, pool):
    mine = [k for k in range(SLOTS) if (k in POOL_LO) == pool]
    return 2 * len(mine) * i + s // SLOTS * len(mine) + sum(k <= s % SLOTS for k in mine)


def proj_slot(j):
    return GROUP_AT[j // 2] + j % 2


def tp_slot(j):
    return 7 + j


def at_slot(place, s, n=PJ):
    return next((j for j in range(n) if place(j) == s), None)


def before(place, s, n=PJ):
    return sum(place(j) < s for j in range(n))


def turn_slot(u):
    return 31 + u


def out_slot(u):
    return (42, 43, 45, 47, 58, 59, 61, 63)[u]


def out_unit(s, place):
    for back in (0, 1):
        if (u := at_slot(place, s + 2 * SLOTS * back)) is not None:
            return back, u
    return None


def out_before(s, place):
    return before(place, s) + before(place, s + 2 * SLOTS) - PJ


class Semaphores:

    def __init__(self, nc, tag):
        self.nc, self.tag, self.made = nc, tag, []

    def __call__(self, name):
        self.made.append(self.nc.alloc_semaphore(name=f"{name}_{self.tag}"))
        return self.made[-1]

    def end(self):
        self.nc.clear_and_free_semaphores(self.made)
        self.nc.all_engine_barrier()


def attention(nc, ctx, io, t):
    es = ExitStack()
    sem = Semaphores(nc, "at")

    def sb(name, shape, dt):
        return es.enter_context(nc.sbuf_tensor(name, shape, dt))

    def ps(name, shape, dt):
        return es.enter_context(nc.psum_tensor(name, shape, dt))

    with es:
        w_hi = sb("w_hi", [P, H * QKV], F16)
        w_lo = sb("w_lo", [P, H * QKV], F16)
        xT_hi = sb("xT_hi", [P, T], F16)
        xT_lo = sb("xT_lo", [P, T], F16)
        wo = sb("wo", [P, H // 2 * D], F32)
        esc = sb("esc", [P, H], F32)
        nesc = sb("nesc", [P, H], F32)
        scl = sb("scl", [P, H], F32)
        cur_esc = sb("cur_esc", [P, 2], F32)
        cur_nesc = sb("cur_nesc", [P, 2], F32)
        raw = sb("raw", [P, 4, 4, QKV], F32)
        sq = sb("sq", [P, 2, 4, 2, DH], F32)
        ss = sb("ss", [P, 2, 4, 2], F32)
        rn = sb("rn", [P, 2, 4, 2], F32)
        nrm = sb("nrm", [P, 2, 4, 2, DH], F32)
        stk = sb("stk", [P, 4, 4, STK], F16)
        QK = sb("QK", [P, 2, 3, T], F16)
        V = sb("V", [P, 2, NT, VW], F16)
        Pr = sb("Pr", [P, PB, KT, QW], F32)
        Pl = sb("Pl", [P, PB, KT, QW], F16)
        rden = sb("rden", [P, 4, 2], F32)
        Or = sb("Or", [P, 4, 258], F32)
        osum = sb("osum", [P, 2, 2, DH], F32)
        Ob = sb("Ob", [P, NT, 2 * DH], F32)
        OT = sb("OT", [P, PJ, 2, P], F32)
        half = sb("mhalf", [P, 1], F32)
        w_f32 = QK[:, 1, :, :].rearrange("p k t -> p (k t)").bitcast(F32)
        xT_f32 = Pr[:, 0:2, :, :].rearrange("p a b c -> p (a b c)")
        ss2 = sb("ss2", [P, 2, 4, 2], F32)

        SC = [ps(f"SC{i}", [P, KT, QW], F32) for i in range(2)]
        OP = [ps(f"OP{i}", [P, 512], F32) for i in range(2)]
        M0 = ps("M0", [P, 512], F32)
        M1 = ps("M1", [P, 512], F32)

        s_ld = {k: sem("s_ld_" + k) for k in ("x", "w", "xt", "wo", "scl")}
        s_init = sem("s_init")
        s_wsp = sem("s_wsp")
        s_xsp = sem("s_xsp")
        s_esc = sem("s_esc")
        s_nesc = sem("s_nesc")
        s_cur = sem("s_cur")
        s_sc = sem("s_sc")
        s_ex = sem("s_ex")
        s_pl = sem("s_pl")
        s_plp = sem("s_plp")
        s_av = sem("s_av")
        s_ob = sem("s_ob")
        s_dv = sem("s_dv")
        s_pj = sem("s_pj")
        s_raw = sem("s_raw")
        s_sq = sem("s_sq")
        s_ss = sem("s_ss")
        s_cl = sem("s_cl")
        s_pw = sem("s_pw")
        s_rn = sem("s_rn")
        s_nrm = sem("s_nrm")
        s_vh = sem("s_vh")
        s_vl = sem("s_vl")
        s_hi = sem("s_hi")
        s_dup = sem("s_dup")
        s_lo = sem("s_lo")
        s_tp = sem("s_tp")
        s_o = sem("s_o")
        s_os = sem("s_os")
        s_ot = sem("s_ot")
        s_ote = sem("s_ote")
        s_y = sem("s_y")
        s_acc = sem("s_acc")
        s_xb = sem("s_xb")
        s_half = sem("s_half")
        s_tpd = sem("s_tpd")
        s_tpa = sem("s_tpa")
        block = es.enter_context(nc.Block())

        def heads(eng, emit):
            for s in range(2 * SLOTS):
                emit(0, s)
            with eng.Fori(1, H // 2 - 1) as i:
                for s in range(2 * SLOTS):
                    emit(i, s)
            for s in range(2 * SLOTS):
                emit(H // 2 - 1, s)
            for s in range(TAIL):
                emit(H // 2, s)

        def ended(i):
            return isinstance(i, int) and i == H // 2

        def prepares(i, s):
            return not (isinstance(i, int) and 2 * i + s // SLOTS >= H - 1)

        def started(i, back):
            return not (isinstance(i, int) and i - back < 0)

        def exists(i, back):
            return started(i, back) and not (ended(i) and not back)

        @block.sync
        def _(eng):
            eng.dma_start(xT_f32, io["xT"]).then_inc(s_ld["xt"], 16)
            eng.dma_start(w_f32, io["wqkv"]).then_inc(s_ld["w"], 16)
            eng.dma_start(scl[:, :], io["scale"].partition_broadcast(P)).then_inc(s_ld["scl"], 16)
            eng.dma_start(wo[:, :], io["wout"]).then_inc(s_ld["wo"], 16)
            eng.dma_start(t["x"][:, :, :], io["x"].rearrange("(t p) d -> p t d", p=P)).then_inc(s_ld["x"], 16)
            eng.dma_start(t["bout"][:, :], io["b_out"].partition_broadcast(P)).then_inc(s_ld["x"], 16)

        @block.tensor
        def _(eng):
            ident16, ident32 = t["ident16"], t["ident32"]

            def m0_free(h, j, i, s):
                wait(eng, s_sq, 8 * h + j)
                wait(eng, s_acc, 8 * i + out_before(s, out_slot))

            def m1_free(h, j, i, s):
                wait(eng, s_tpd, 4 * h + (j + 1) // 2)
                wait(eng, s_tpa, 4 * h + j // 2)
                wait(eng, s_ote, 8 * i + out_before(s, turn_slot))

            def proj(h, j):
                for r in range(2):
                    tile = 2 * j + r
                    out = M0[:, QKV * r:QKV * r + QKV]
                    hi, lo = xT_hi[:, P * tile:P * tile + P], xT_lo[:, P * tile:P * tile + P]
                    wh, wl = w_hi[:, bass.ds(QKV * h, QKV)], w_lo[:, bass.ds(QKV * h, QKV)]
                    eng.matmul(out, hi, wh, start=True, stop=False)
                    eng.matmul(out, hi, wl, start=False, stop=False)
                    mm = eng.matmul(out, lo, wh, start=False, stop=True)
                mm.then_inc(s_pj, 1)

            def transposes(h, j):
                g = j // 2
                wait(eng, s_hi, 4 * h + g + 1)
                wait(eng, s_dup, 4 * h + g + 1)
                wait(eng, s_lo, 4 * h + g + 1)
                m1 = M1[:, :].bitcast(F16)
                for kind in range(3):
                    at = (0, 2 * DH, 3 * DH)[kind]
                    for r in range(2):
                        mm = eng.transpose(m1[:, (2 * kind + r) * P:(2 * kind + r + 1) * P],
                                           stk[:, g, 2 * (j % 2) + r, at:at + P], ident16[:, :])
                mm.then_inc(s_tp, 1)

            def scores(i, s):
                n, h, b = 32 * i + s, 2 * i + s // SLOTS, s // SLOTS
                s %= SLOTS
                bat, q, kh = s // 8, s % 8 // 2, s % 2
                if s == 0:
                    wait(eng, s_tpd, 4 * h + 4)
                    wait(eng, s_tpa, 4 * h + 4)
                wait(eng, s_ex, n - 1)
                for kt in range(KT):
                    key = bat * S + (kh * KT + kt) * P
                    rhs = QK[:, b, 0, bat * S + q * QW:bat * S + q * QW + QW]
                    out = SC[s % 2][:, kt, :]
                    eng.matmul(out, QK[:, b, 1, key:key + P], rhs, start=True, stop=False)
                    mm = eng.matmul(out, QK[:, b, 2, key:key + P], rhs, start=False, stop=True)
                mm.then_inc(s_sc, 1)

            def av(i, s):
                n, h, b = 32 * i + s, 2 * i + s // SLOTS, s // SLOTS
                s %= SLOTS
                bat, kh, u = s // 8, s % 2, s // 2
                pool = s in POOL_LO
                wait(eng, s_plp if pool else s_pl, low_count(i, s + SLOTS * b, pool))
                if s == 0:
                    wait(eng, s_vh, 4 * h + 4)
                    wait(eng, s_vl, 4 * h + 4)
                if kh == 0:
                    wait(eng, s_ob, 16 * i + 8 * b + u - 1)
                for kt in range(KT):
                    tile = bat * 8 + kh * KT + kt
                    for r in range(2):
                        hi = high(Pr[:, s % PB, kt, P * r:P * r + P])[:, 1::2]
                        lo = Pl[:, s % PB, kt, P * r:P * r + P]
                        at = 129 * r
                        first = kh == 0 and kt == 0 and r == 0
                        last = kh == 1 and kt == KT - 1 and r == 1
                        eng.matmul(OP[u % 2][:, at:at + 129], hi, V[:, b, tile, 0:129],
                                   start=first, stop=False, skip_group_check=True)
                        mm = eng.matmul(OP[u % 2][:, at:at + 65], lo, V[:, b, tile, 0:65],
                                        start=False, stop=last, skip_group_check=True)
                mm.then_inc(s_av, 1)

            def out_transposes(i, u):
                wait(eng, s_o, 16 * i + 8 + u + 1)
                for r in range(2):
                    mm = eng.transpose(M1[:, P * r:P * r + P], Ob[:, 2 * u + r, :], ident32[:, :])
                mm.then_inc(s_ot, 1)

            def out_product(i, u):
                wait(eng, s_ote, 8 * i + u + 1)
                for r in range(2):
                    mm = eng.matmul(M0[:, P * r:P * r + P], OT[:, u, r, :],
                                    wo[:, bass.ds(D * i, D)], start=True, stop=True)
                mm.then_inc(s_y, 1)

            def slot(i, s):
                h, sh = 2 * i + s // SLOTS, s % SLOTS
                pj, tp = before(proj_slot, sh), before(tp_slot, sh)
                if not prepares(i, s):
                    pj, tp = (0, 0) if ended(i) or s >= SLOTS else (pj, tp)
                nh = H if not prepares(i, s) else h + 1
                if not ended(i):
                    scores(i, s)
                if s >= LAG and not ended(i):
                    av(i, s - LAG)
                elif s < LAG and started(i, 1):
                    av(i - 1, s + 2 * SLOTS - LAG)
                if (x := out_unit(s, turn_slot)) and exists(i, x[0]):
                    m1_free(nh, tp, i, s)
                    out_transposes(i - x[0], x[1])
                if (x := out_unit(s, out_slot)) and exists(i, x[0]):
                    m0_free(nh, pj, i, s)
                    out_product(i - x[0], x[1])
                if prepares(i, s):
                    if (j := at_slot(proj_slot, sh)) is not None:
                        m0_free(h + 1, j, i, s)
                        proj(h + 1, j)
                    if (j := at_slot(tp_slot, sh)) is not None:
                        m1_free(h + 1, j, i, s)
                        transposes(h + 1, j)

            eng.wait_ge(s_wsp, 2 * WCH)
            eng.wait_ge(s_xsp, 2)
            eng.wait_ge(t["s_ident"], 4)
            for s in range(SLOTS):
                if (j := at_slot(proj_slot, s)) is not None:
                    m0_free(0, j, 0, 0)
                    proj(0, j)
                if (j := at_slot(tp_slot, s)) is not None:
                    m1_free(0, j, 0, 0)
                    transposes(0, j)
            eng.wait_ge(s_ld["wo"], 16)
            heads(eng, slot)

        @block.scalar
        def _(eng):
            def read_proj(h, hb, j):
                J, G, g, b = 8 * h + j, 4 * h + j // 2, j // 2, j // 2 % 2
                r = 2 * (j % 2)
                wait(eng, s_pj, J + 1)
                if j % 2 == 0:
                    wait(eng, s_nrm, G - 3)
                    wait(eng, s_vl, G - 3)
                    wait(eng, s_ss, G - 1)
                m0 = M0[:, 0:2 * QKV].rearrange("p (r c) -> p r c", r=2)
                eng.activation(raw[:, g, r:r + 2, :], m0, ACT.Copy).then_inc(s_raw, 1)
                eng.activation(sq[:, b, r:r + 2, :, :], m0[:, :, 0:2 * DH].rearrange("p r (k d) -> p r k d", k=2),
                               ACT.Square).then_inc(s_sq, 1)

            def high_values(h, hb, g):
                wait(eng, s_raw, 8 * h + 2 * g + 2)
                wait(eng, s_av, SLOTS * (h - 1))
                eng.activation(V[:, hb, 4 * g:4 * g + 4, 0:DH], raw[:, g, :, 2 * DH:QKV], ACT.Copy).then_inc(s_vh, 1)

            def read_transposes(h, hb, j):
                wait(eng, s_tp, 8 * h + j + 1)
                eng.activation(QK[:, hb, :, 2 * P * j:2 * P * j + 2 * P],
                               M1[:, :].bitcast(F16)[:, 0:6 * P].rearrange("p (k c) -> p k c", k=3),
                               ACT.Copy).then_inc(s_tpa, 1)

            def read_out_transposes(i, u):
                wait(eng, s_ot, 8 * i + u + 1)
                eng.activation(OT[:, u, :, :], M1[:, 0:2 * P].rearrange("p (r c) -> p r c", r=2), ACT.Copy).then_inc(s_ote, 1)

            def read_out(i, s):
                b, u = s // SLOTS, s % SLOTS // 2
                m = 16 * i + 8 * b + u
                wait(eng, s_av, 2 * m + 2)
                wait(eng, s_o, m - 3)
                eng.activation(Or[:, u % 4, :], OP[u % 2][:, 0:258], ACT.Copy).then_inc(s_ob, 1)

            def exps(i, s):
                n, b = 32 * i + s, s // SLOTS
                if s % SLOTS == 0:
                    wait(eng, s_cur, 4 * i + 2 * b + 2)
                wait(eng, s_sc, n + 1)
                wait(eng, s_av, n - PB + 1)
                eng.activation(Pr[:, s % PB, :, :], SC[s % 2][:, :, :], ACT.Exp,
                               bias=cur_nesc[:, b:b + 1]).then_inc(s_ex, 1)

            def slot(i, s):
                h, sh = 2 * i + s // SLOTS, s % SLOTS
                if not ended(i):
                    exps(i, s)
                if (x := out_unit(s, turn_slot)) and exists(i, x[0]):
                    read_out_transposes(i - x[0], x[1])
                if s % 2 == 0:
                    if s >= 4 and not ended(i):
                        read_out(i, s - 4)
                    elif s < 4 and started(i, 1):
                        read_out(i - 1, s + 2 * SLOTS - 4)
                if prepares(i, s):
                    prepare(h + 1, (s // SLOTS + 1) % 2, sh)

            def prepare(h, hb, s):
                if (j := at_slot(proj_slot, s)) is not None:
                    read_proj(h, hb, j)
                if (g := at_slot(lambda g: GROUP_AT[g] + 2, s, 4)) is not None:
                    high_values(h, hb, g)
                if (j := at_slot(tp_slot, s)) is not None and j % 2:
                    read_transposes(h, hb, j)

            eng.wait_ge(s_ld["scl"], 16)
            eng.activation(esc[:, :], scl[:, :], ACT.Exp).then_inc(s_esc, 1)
            for s in range(SLOTS):
                prepare(0, 0, s)
            heads(eng, slot)

        @block.vector
        def _(eng):
            def square_sums(h, hb, g):
                G, b = 4 * h + g, g % 2
                wait(eng, s_sq, 8 * h + 2 * g + 2)
                eng.tensor_reduce(ss[:, b, :, :], sq[:, b, :, :, :], AX, ALU.add).then_inc(s_ss, 1)
                wait(eng, s_ss, G + 1)
                wait(eng, s_pw, G - 1)
                eng.tensor_scalar(ss2[:, b, :, :], ss[:, b, :, :], 1e-24, None, ALU.max).then_inc(s_cl, 1)

            def normalize(h, hb, g):
                G, b = 4 * h + g, g % 2
                wait(eng, s_rn, G + 1)
                wait(eng, s_raw, 8 * h + 2 * g + 2)
                wait(eng, s_hi, G - 1)
                wait(eng, s_lo, G - 1)
                qk = raw[:, g, :, 0:2 * DH].rearrange("p t (k d) -> p t k d", k=2)
                eng.tensor_tensor(nrm[:, b, :, :, :], qk, rn[:, b, :, :].unsqueeze(3).to_broadcast([P, 4, 2, DH]),
                                  ALU.mult).then_inc(s_nrm, 1)

            def high_parts(h, hb, g):
                G, b = 4 * h + g, g % 2
                wait(eng, s_nrm, G + 1)
                wait(eng, s_tp, 8 * (h - 1) + 2 * g + 2)
                out = stk[:, g, :, 0:4 * DH].rearrange("p t (k x) -> p t k x", k=2)[:, :, :, 0:DH]
                eng.tensor_copy(out, nrm[:, b, :, :, :]).then_inc(s_hi, 1)

            def copy_keys(h, hb, g):
                G, b = 4 * h + g, g % 2
                wait(eng, s_hi, G + 1)
                eng.tensor_copy(stk[:, g, :, 4 * DH:5 * DH], stk[:, g, :, 2 * DH:3 * DH]).then_inc(s_dup, 1)

            def read_transposes(h, hb, j):
                wait(eng, s_tp, 8 * h + j + 1)
                eng.tensor_copy(QK[:, hb, :, 2 * P * j:2 * P * j + 2 * P].bitcast(U32),
                                M1[:, 0:3 * P].bitcast(U32).rearrange("p (k c) -> p k c", k=3)).then_inc(s_tpd, 1)

            def low_probs(i, s):
                n = 32 * i + s
                wait(eng, s_ex, n + 1)
                wait(eng, s_av, n - PB + 1)
                pr = Pr[:, s % PB, :, :].rearrange("p a b -> p (a b)")
                eng.tensor_tensor(Pl[:, s % PB, :, :].rearrange("p a b -> p (a b)"), pr, high(pr)[:, 1::2],
                                  ALU.subtract).then_inc(s_pl, 1)

            def inverse_sums(i, s):
                b, u = s // SLOTS, s % SLOTS // 2
                m = 16 * i + 8 * b + u
                wait(eng, s_ob, m + 1)
                wait(eng, s_o, m - 3)
                eng.reciprocal(rden[:, u % 4, :], Or[:, u % 4, DH:DH + 130:129]).then_inc(s_dv, 1)

            def add_out(i, u):
                wait(eng, s_y, 8 * i + u + 1)
                acc = t["x"][:, 2 * u:2 * u + 2, :]
                eng.tensor_tensor(acc, acc, M0[:, 0:2 * P].rearrange("p (r c) -> p r c", r=2),
                                  ALU.add).then_inc(s_acc, 1)

            def head_scale(b, h):
                eng.tensor_copy(cur_esc[:, b:b + 1], esc[:, bass.ds(h, 1)]).then_inc(s_cur, 1)
                eng.tensor_scalar(cur_nesc[:, b:b + 1], esc[:, bass.ds(h, 1)], -1.0, None, ALU.mult).then_inc(s_cur, 1)

            def prepare(h, hb, s):
                if (j := at_slot(tp_slot, s)) is not None and j % 2 == 0:
                    read_transposes(h, hb, j)
                if s == 0:
                    head_scale(hb, h)
                if (g := at_slot(lambda g: GROUP_AT[g] + 2, s, 4)) is not None:
                    square_sums(h, hb, g)
                if (g := at_slot(lambda g: GROUP_AT[g] + 3, s, 4)) is not None:
                    normalize(h, hb, g)
                    high_parts(h, hb, g)
                    copy_keys(h, hb, g)

            def slot(i, s):
                h, sh = 2 * i + s // SLOTS, s % SLOTS
                if not ended(i) and sh not in POOL_LO:
                    low_probs(i, s)
                if (x := out_unit(s, out_slot)) and exists(i, x[0]):
                    add_out(i - x[0], x[1])
                if prepares(i, s):
                    prepare(h + 1, (s // SLOTS + 1) % 2, sh)
                if s % 2 == 0:
                    if s >= 4 and not ended(i):
                        inverse_sums(i, s - 4)
                    elif s < 4 and started(i, 1):
                        inverse_sums(i - 1, s + 2 * SLOTS - 4)


            eng.memset(V[:, :, :, DH:DH + 1], 1.0).then_inc(s_init, 1)
            eng.wait_ge(s_ld["xt"], 16)
            eng.tensor_copy(xT_hi[:, :], xT_f32).then_inc(s_xsp, 1)
            eng.wait_ge(s_xsp, 1)
            eng.tensor_tensor(xT_lo[:, :], xT_f32, xT_hi[:, :], ALU.subtract).then_inc(s_xsp, 1)
            eng.wait_ge(s_ld["w"], 16)
            for c in range(WCH):
                cs = slice(c * H * QKV // WCH, (c + 1) * H * QKV // WCH)
                eng.tensor_copy(w_hi[:, cs], w_f32[:, cs]).then_inc(s_wsp, 1)
                eng.wait_ge(s_wsp, 2 * c + 1)
                eng.tensor_tensor(w_lo[:, cs], w_f32[:, cs], w_hi[:, cs], ALU.subtract).then_inc(s_wsp, 1)
            eng.wait_ge(s_ld["x"], 32)
            eng.tensor_tensor(t["x"][:, :, :], t["x"][:, :, :],
                              t["bout"][:, :].unsqueeze(1).to_broadcast([P, NT, D]), ALU.add).then_inc(s_xb, 1)
            eng.wait_ge(s_esc, 1)
            for s in range(SLOTS):
                prepare(0, 0, s)
            eng.wait_ge(s_xb, 1)
            heads(eng, slot)

        @block.gpsimd
        def _(eng):
            def low_probs(i, s):
                n = 32 * i + s
                wait(eng, s_ex, n + 1)
                wait(eng, s_av, n - PB + 1)
                pr = Pr[:, s % PB, :, :].rearrange("p a b -> p (a b)")
                eng.tensor_tensor(Pl[:, s % PB, :, :].rearrange("p a b -> p (a b)"), pr, high(pr)[:, 1::2],
                                  ALU.subtract).then_inc(s_plp, 1)

            def divide(i, s):
                b, u = s // SLOTS, s % SLOTS // 2
                m = 16 * i + 8 * b + u
                wait(eng, s_ob, m + 1)
                o = Or[:, u % 4, :].rearrange("p (r c) -> p r c", r=2)
                eng.tensor_tensor(osum[:, u % 2, :, :], o[:, :, 0:DH], o[:, :, DH + 1:], ALU.add).then_inc(s_os, 1)
                wait(eng, s_os, m + 1)
                wait(eng, s_dv, m + 1)
                eng.tensor_tensor(Ob[:, 2 * u:2 * u + 2, DH * b:DH * b + DH], osum[:, u % 2, :, :],
                                  rden[:, u % 4, :].unsqueeze(2).to_broadcast([P, 2, DH]), ALU.mult).then_inc(s_o, 1)

            def inverse_norms(h, hb, g):
                G, b = 4 * h + g, g % 2
                wait(eng, s_cl, G + 1)
                wait(eng, s_nrm, G - 1)
                eng.tensor_tensor(rn[:, b, :, :], ss2[:, b, :, :],
                                  half[:, 0:1].unsqueeze(2).to_broadcast([P, 4, 2]), ALU.pow).then_inc(s_pw, 1)
                wait(eng, s_pw, G + 1)
                wait(eng, s_cur, 2 * h + 1)
                eng.tensor_tensor(rn[:, b, :, 0], rn[:, b, :, 0],
                                  cur_esc[:, hb:hb + 1].to_broadcast([P, 4]), ALU.mult).then_inc(s_rn, 1)

            def low_values(h, hb, g):
                G, b = 4 * h + g, g % 2
                wait(eng, s_raw, 8 * h + 2 * g + 2)
                wait(eng, s_vh, G + 1)
                v = V[:, hb, 4 * g:4 * g + 4, :]
                eng.tensor_tensor(v[:, :, DH + 1:2 * DH + 1], raw[:, g, :, 2 * DH:QKV], v[:, :, 0:DH],
                                  ALU.subtract).then_inc(s_vl, 1)

            def low_parts(h, hb, g):
                G, b = 4 * h + g, g % 2
                wait(eng, s_hi, G + 1)
                both = stk[:, g, :, 0:4 * DH].rearrange("p t (k x) -> p t k x", k=2)
                eng.tensor_tensor(both[:, :, :, DH:2 * DH], nrm[:, b, :, :, :], both[:, :, :, 0:DH],
                                  ALU.subtract).then_inc(s_lo, 1)

            def prepare(h, hb, s):
                if (g := at_slot(lambda g: GROUP_AT[g] + 2, s, 4)) is not None:
                    inverse_norms(h, hb, g)
                    low_values(h, hb, g)
                if (g := at_slot(lambda g: GROUP_AT[g] + 3, s, 4)) is not None:
                    low_parts(h, hb, g)

            def slot(i, s):
                h, sh = 2 * i + s // SLOTS, s % SLOTS
                if not ended(i) and sh in POOL_LO:
                    low_probs(i, s)
                if prepares(i, s):
                    prepare(h + 1, (s // SLOTS + 1) % 2, sh)
                if s % 2 == 0:
                    if s >= 4 and not ended(i):
                        divide(i, s - 4)
                    elif s < 4 and started(i, 1):
                        divide(i - 1, s + 2 * SLOTS - 4)

            for m in (t["ident16"], t["ident32"]):
                eng.memset(m[:, :], 0.0).then_inc(t["s_ident"], 1)
            eng.memset(half[:, :], -0.5).then_inc(s_half, 1)
            eng.wait_ge(t["s_ident"], 2)
            for m in (t["ident16"], t["ident32"]):
                eng.affine_select(out=m[:, :], in_=m[:, :], compare_op=ALU.not_equal, fill=1.0, base=0,
                                  pattern=[[-1, P]], channel_multiplier=1).then_inc(t["s_ident"], 1)
            eng.wait_ge(s_half, 1)
            for s in range(SLOTS):
                prepare(0, 0, s)
            heads(eng, slot)

    sem.end()


TB = NT // B
G2 = 2
TG = S // G2


def normalize_and_turn(nc, tag, t, io, jobs, layer=None):
    es = ExitStack()
    sem = Semaphores(nc, tag)
    with es:
        def sb(name, shape, dt):
            return es.enter_context(nc.sbuf_tensor(f"{name}_{tag}", shape, dt))

        x, xT, xl = t["x"], t["xT"], t["xl"]
        stats = sb("stats", [P, B, TB, 6], F32)
        mv = sb("mv", [P, B, TB, 2], F32)
        ve = sb("ve", [P, B, TB], F32)
        rstd = sb("rstd", [P, B, TB], F32)
        lg = sb("lg", [P, B, TB, E], F32)
        mx = sb("mx", [P, B, TB, 8], F32)
        ix = sb("ix", [P, B, TB, 8], U32)
        ixf = sb("ixf", [P, B, TB, 2], F32)
        df = sb("df", [P, B, TB], F32)
        ex = sb("ex", [P, B, TB], F32)
        e1 = sb("e1", [P, B, TB], F32)
        p1 = sb("p1", [P, B, TB], F32)
        p2 = sb("p2", [P, B, TB], F32)
        m1 = sb("m1", [P, B, TB, E], F32)
        m2 = sb("m2", [P, B, TB, E], F32)
        YT = [es.enter_context(nc.psum_tensor(f"YT{i}_{tag}", [P, 4, P], F32)) for i in range(2)]
        XT = [es.enter_context(nc.psum_tensor(f"XT{i}_{tag}", [P, 4, P], F32)) for i in range(4)]
        LG = [es.enter_context(nc.psum_tensor(f"LG{i}_{tag}", [P, TB, E], F32)) for i in range(2)]

        s_yt, s_add, s_st, s_mv, s_ve, s_rs, s_xn, s_tp, s_xt, s_xl, s_out = (
            sem(n) for n in ("g_yt", "g_add", "g_st", "g_mv", "g_ve", "g_rs", "g_xn", "g_tp", "g_xt", "g_xl", "g_out"))
        s_w = [sem(f"g_w{k}") for k in range(2)]
        s_wh, s_wl = sem("g_wh"), sem("g_wl")
        s_lg, s_lc, s_mx, s_ix, s_df, s_ex, s_e1, s_p1, s_p2, s_eq, s_ml, s_cw = (
            sem(n) for n in ("g_lg", "g_lc", "g_mx", "g_ix", "g_df", "g_ex", "g_e1", "g_p1", "g_p2", "g_eq",
                             "g_ml", "g_cw"))
        block = es.enter_context(nc.Block())
        turned = [(n, b, route) for n, (b, _, route, store) in enumerate(jobs) if store is None]
        routed = [(n, b) for n, b, route in turned if route]
        W = 0 if layer is None else (3, 2)[layer] * FF

        @block.sync
        def _(eng):
            if W:
                for k in range(2):
                    eng.dma_start(t["wf"][:, k, 0:W], io[f"w{layer}"][:, W * k:W * k + W]).then_inc(s_w[k], 16)
            for n, (b, _, _, store) in enumerate(jobs):
                if store is not None:
                    rows = store.rearrange("(t p) d -> p t d", p=P)
                    for k in range(0, TB, TB // 2):
                        eng.wait_ge(s_xn, TB * n + k + TB // 2)
                        eng.dma_start(rows[:, k:k + TB // 2, :],
                                      x[:, TB * b + k:TB * b + k + TB // 2, :]).then_inc(s_out, 16)
            if jobs[-1][3] is not None:
                eng.wait_ge(s_out, 32)
            if W:
                for k in range(2):
                    eng.wait_ge(s_w[k], 16)

        @block.tensor
        def _(eng):
            for n, (b, adds, _, _) in enumerate(jobs):
                if adds:
                    for k in range(2):
                        for r in range(4):
                            mm = eng.transpose(YT[k][:, r, :], t[adds][:, b, (4 * k + r) * P:(4 * k + r + 1) * P],
                                               t["ident32"][:, :])
                        mm.then_inc(s_yt, 1)
            for n, b, route in turned:
                for k in range(2):
                    eng.wait_ge(s_xn, TB * n + 4 * k + 4)
                    for r in range(4):
                        mm = eng.transpose(XT[2 * n + k][:, r, :], x[:, TB * b + 4 * k + r, :], t["ident32"][:, :])
                    mm.then_inc(s_tp, 1)
                if route:
                    for k in range(TB):
                        if k % 4 == 0:
                            eng.wait_ge(s_xt, 2 * n + k // 4 + 1)
                        col = b * S + k * P
                        mm = eng.matmul(LG[n][:, k, :], xT[:, col:col + P], t[route][:, :], start=True, stop=True)
                    mm.then_inc(s_lg, 1)

        @block.scalar
        def _(eng):
            if W:
                eng.wait_ge(s_w[0], 16)
                eng.activation(t["wh"][:, 0, 0:W], t["wf"][:, 0, 0:W], ACT.Copy).then_inc(s_wh, 1)
            for n, b, _ in turned:
                for k in range(2):
                    eng.wait_ge(s_tp, 2 * n + k + 1)
                    col = b * S + 4 * k * P
                    eng.activation(xT[:, col:col + 4 * P], XT[2 * n + k][:, :, :].rearrange("p r c -> p (r c)"),
                                   ACT.Copy).then_inc(s_xt, 1)
            for n, b in routed:
                eng.wait_ge(s_df, n + 1)
                eng.activation(ex[:, b, :], df[:, b, :], ACT.Exp).then_inc(s_ex, 1)

        @block.gpsimd
        def _(eng):
            for n, (b, _, _, _) in enumerate(jobs):
                eng.wait_ge(s_ve, n + 1)
                eng.tensor_tensor(rstd[:, b, :], ve[:, b, :], t["half"][:, 0:1].to_broadcast([P, TB]),
                                  ALU.pow).then_inc(s_rs, 1)
            if W:
                eng.wait_ge(s_wh, 1)
                eng.tensor_tensor(t["wl"][:, 0, 0:W], t["wf"][:, 0, 0:W], t["wh"][:, 0, 0:W],
                                  ALU.subtract).then_inc(s_wl, 1)

        @block.vector
        def _(eng):
            def statistics(n, b, adds):
                if adds:
                    for k in range(2):
                        eng.wait_ge(s_yt, k + 1)
                        xs = x[:, TB * b + 4 * k:TB * b + 4 * k + 4, :]
                        eng.tensor_tensor(xs, xs, YT[k][:, :, :], ALU.add).then_inc(s_add, 1)
                for k in range(TB):
                    if adds and k % 4 == 0:
                        eng.wait_ge(s_add, k // 4 + 1)
                    eng.bn_stats(stats[:, b, k, :], x[:, TB * b + k, :]).then_inc(s_st, 1)
                for k in range(TB):
                    eng.wait_ge(s_st, TB * n + k + 1)
                    eng.bn_aggr(mv[:, b, k, :], stats[:, b, k, :]).then_inc(s_mv, 1)
                eng.wait_ge(s_mv, TB * (n + 1))
                eng.tensor_scalar(ve[:, b, :], mv[:, b, :, 1], EPS, None, ALU.add).then_inc(s_ve, 1)

            def rows(n, b):
                eng.wait_ge(s_rs, n + 1)
                for k in range(TB):
                    xs = x[:, TB * b + k, :]
                    eng.tensor_scalar(xs, xs, mv[:, b, k, 0:1], rstd[:, b, k:k + 1], ALU.subtract,
                                      ALU.mult).then_inc(s_xn, 1)

            def low(n, b):
                for k in range(2):
                    eng.wait_ge(s_xt, 2 * n + k + 1)
                    xs = xT[:, b * S + 4 * k * P:b * S + 4 * (k + 1) * P]
                    eng.tensor_tensor(xl[:, b * S + 4 * k * P:b * S + 4 * (k + 1) * P], xs, high(xs)[:, 1::2],
                                      ALU.subtract).then_inc(s_xl, 1)

            def choose(n, b):
                eng.wait_ge(s_lg, n + 1)
                eng.tensor_copy(lg[:, b, :, :], LG[n][:, :, :]).then_inc(s_lc, 1)
                eng.wait_ge(s_lc, n + 1)
                for k in range(TB):
                    eng.max(mx[:, b, k, :], lg[:, b, k, :]).then_inc(s_mx, 1)
                eng.wait_ge(s_mx, TB * (n + 1))
                eng.tensor_tensor(df[:, b, :], mx[:, b, :, 1], mx[:, b, :, 0], ALU.subtract).then_inc(s_df, 1)
                for k in range(TB):
                    eng.max_index(ix[:, b, k, :], mx[:, b, k, :], lg[:, b, k, :]).then_inc(s_ix, 1)
                eng.wait_ge(s_ix, (TB + 1) * n + TB)
                eng.tensor_copy(ixf[:, b, :, :], ix[:, b, :, 0:2]).then_inc(s_ix, 1)

            def combine(n, b):
                eng.wait_ge(s_ex, n + 1)
                eng.tensor_scalar(e1[:, b, :], ex[:, b, :], 1.0, None, ALU.add).then_inc(s_e1, 1)
                eng.wait_ge(s_e1, n + 1)
                eng.reciprocal(p1[:, b, :], e1[:, b, :]).then_inc(s_p1, 1)
                iota = t["iota"][:, :].unsqueeze(1).to_broadcast([P, TB, E])
                for k, m in enumerate((m1, m2)):
                    eng.tensor_tensor(m[:, b, :, :], iota, ixf[:, b, :, k:k + 1].to_broadcast([P, TB, E]),
                                      ALU.is_equal).then_inc(s_eq, 1)
                eng.wait_ge(s_p1, n + 1)
                eng.tensor_tensor(p2[:, b, :], ex[:, b, :], p1[:, b, :], ALU.mult).then_inc(s_p2, 1)
                eng.wait_ge(s_p2, n + 1)
                eng.wait_ge(s_eq, 2 * n + 2)
                for m, pr in ((m1, p1), (m2, p2)):
                    eng.tensor_tensor(m[:, b, :, :], m[:, b, :, :],
                                      pr[:, b, :].unsqueeze(2).to_broadcast([P, TB, E]), ALU.mult).then_inc(s_ml, 1)
                eng.wait_ge(s_ml, 2 * n + 2)
                eng.tensor_tensor(t["cw"][:, TB * b:TB * b + TB, 0:E], m1[:, b, :, :], m2[:, b, :, :],
                                  ALU.add).then_inc(s_cw, 1)

            for n, (b, adds, _, _) in enumerate(jobs):
                statistics(n, b, adds)
            for n, (b, _, _, _) in enumerate(jobs):
                rows(n, b)
            for n, b, route in turned:
                low(n, b)
                if route:
                    choose(n, b)
            for n, b in routed:
                eng.wait_ge(s_ix, (TB + 1) * (n + 1))
                combine(n, b)

    sem.end()


def prepare_rest(nc, t, io):
    es = ExitStack()
    sem = Semaphores(nc, "pr")
    with es:
        def sb(name, shape, dt):
            return es.enter_context(nc.sbuf_tensor(name, shape, dt))

        al, ab, na, en, ln, mxa = (sb("c_" + n, [P, 16], F32) for n in ("al", "ab", "na", "en", "ln", "mxa"))
        bb, cc = sb("c_b", [P, 16], F32), sb("c_c", [P, 16], F32)
        io_i = sb("io_i", [P, E], mybir.dt.int32)
        s_d, s_i, s_v, s_a = sem("c_d"), sem("c_i"), sem("c_v"), sem("c_a")
        block = es.enter_context(nc.Block())

        @block.sync
        def _(eng):
            for dst, name in ((al[:, :], "a_log"), (bb[:, :], "b"), (cc[:, :], "c"), (t["dtw"][:, :], "dtwT"),
                              (t["dtb"][:, :], "dt_b"), (t["cvw"][:, :], "conv_w"), (t["cvb"][:, :], "conv_b"),
                              (t["gate"][:, :], "gateT"), (t["router"][:, :], "routerT")):
                eng.dma_start(dst, io[name]).then_inc(s_d, 16)
            eng.wait_ge(s_d, 16 * 9)

        @block.gpsimd
        def _(eng):
            eng.iota(io_i[:, :], pattern=[[1, E]], base=0, channel_multiplier=0).then_inc(s_i, 1)
            eng.memset(t["half"][:, :], -0.5).then_inc(s_i, 1)
            eng.memset(t["cw"][:, :, E:E + 1], 1.0).then_inc(s_i, 1)
            eng.wait_ge(s_i, 3)
            eng.tensor_copy(t["iota"][:, :], io_i[:, :]).then_inc(s_i, 1)

        @block.vector
        def _(eng):
            eng.wait_ge(s_d, 16 * 9)
            eng.tensor_scalar(na[:, :], al[:, :], -1.0, None, ALU.mult).then_inc(s_v, 1)
            eng.tensor_tensor(t["bc"][:, :], bb[:, :], cc[:, :], ALU.mult).then_inc(s_v, 1)
            eng.tensor_scalar(mxa[:, :], al[:, :], 0.0, None, ALU.max).then_inc(s_v, 1)
            eng.wait_ge(s_v, 3)
            eng.tensor_tensor(ab[:, :], al[:, :], na[:, :], ALU.min).then_inc(s_v, 1)
            eng.wait_ge(s_a, 2)
            eng.tensor_tensor(na[:, :], mxa[:, :], ln[:, :], ALU.add).then_inc(s_v, 1)
            eng.wait_ge(s_v, 5)
            eng.tensor_scalar(t["A"][:, :], na[:, :], -1.0, None, ALU.mult).then_inc(s_v, 1)

        @block.scalar
        def _(eng):
            eng.wait_ge(s_v, 4)
            eng.activation(en[:, :], ab[:, :], ACT.Exp).then_inc(s_a, 1)
            eng.wait_ge(s_a, 1)
            eng.activation(ln[:, :], en[:, :], ACT.Ln, bias=1.0).then_inc(s_a, 1)

    sem.end()


DS = 16


def experts(nc, tag, t, io, layer, b, ssm):
    NE = E + layer
    W = (3, 2)[layer] * FF
    DOWN = (2, 1)[layer] * FF
    es = ExitStack()
    sem = Semaphores(nc, tag)
    with es:
        def sb(name, shape, dt):
            return es.enter_context(nc.sbuf_tensor(f"{name}_{tag}", shape, dt))

        x, xT, xl, cw = t["x"], t["xT"], t["xl"], t["cw"]
        wf, wh, wl = (t[n][:, :, 0:W] for n in ("wf", "wh", "wl"))
        act = sb("act", [P, NC, TG], F32)
        hid = sb("hid", [P, 2, NC, TG], F32)
        hlo = sb("hlo", [P, 2, NC, TG], F16)
        GB = [es.enter_context(nc.psum_tensor(f"GB{i}_{tag}", [P, TG], F32)) for i in range(2)]
        UB = [es.enter_context(nc.psum_tensor(f"UB{i}_{tag}", [P, TG], F32)) for i in range(4)]
        DB = [es.enter_context(nc.psum_tensor(f"DB{i}_{tag}", [P, 4, P], F32)) for i in range(2)]
        FB = GB if layer == 0 else UB
        NF = len(FB)
        if ssm is not None:
            xf = sb("xf", [P, S], F32)
            sg = sb("sg", [P, S], F32)
            dt = sb("dt", [P, S], F32)
            us = sb("us", [P, S], F32)
            ea = sb("ea", [P, 2, S], F32)
            bu = sb("bu", [P, 2, S], F32)
            st = sb("st", [P, 2, S], F32)

        s_w = [sem(f"w{i}") for i in range(2)]
        (s_wh, s_wl, s_gu, s_act, s_hid, s_lo, s_dn, s_ac, s_xf, s_dtp, s_sg, s_dt, s_us, s_ea, s_bu, s_st,
         s_y) = (sem(n) for n in ("wh", "wl", "gu", "act", "hid", "lo", "dn", "ac", "xf", "dtp", "sg", "dt",
                                  "us", "ea", "bu", "st", "y"))
        block = es.enter_context(nc.Block())
        w_io = io[f"w{layer}"]

        def each(eng, emit, end=None):
            for k in range(2):
                emit(0, k)
            with eng.Fori(1, (NE - 1) // 2) as i:
                for k in range(2):
                    emit(i, k)
            for e in range(2 * ((NE - 1) // 2), NE):
                emit(e // 2, e % 2)
            if end:
                end()

        def states(i, k, g):
            if ssm is None or isinstance(i, int) and (i == E // 2 or i + k + g == 0):
                return ()
            return (0, 1) if isinstance(i, int) and i + k == 0 else (2 * k + g,)

        @block.sync
        def _(eng):
            def load(i, k):
                if isinstance(i, int) and i == 0:
                    return
                wait(eng, s_wh, 2 * i + k - 2)
                wait(eng, s_wl, 2 * i + k - 2)
                eng.dma_start(wf[:, k, :], w_io[:, bass.ds(W * (2 * i + k), W)]).then_inc(s_w[k], 16)

            each(eng, load)

        @block.tensor
        def _(eng):
            def unit(i, k, g, c):
                U = 16 * i + 8 * k + 4 * g + c
                e = 2 * i + k
                if g == 0 and c == 0:
                    wait(eng, s_wh, e)
                    wait(eng, s_wl, e)
                wait(eng, s_act, U - NF + 1)
                if layer == 0:
                    wait(eng, s_hid, U - 3)
                col = b * S + g * TG
                xh, xlo = high(xT[:, col:col + TG])[:, 1::2], xl[:, col:col + TG]
                for m, bank in enumerate((FB[c % NF], UB[c])[:2 - layer]):
                    at = m * FF + P * c
                    eng.matmul(bank[:, :], wh[:, k, at:at + P], xh, start=True, stop=False)
                    eng.matmul(bank[:, :], wl[:, k, at:at + P], xh, start=False, stop=False)
                    mm = eng.matmul(bank[:, :], wh[:, k, at:at + P], xlo, start=False, stop=True)
                mm.then_inc(s_gu, 1)

            def down(i, k, g, tile):
                Q = 4 * i + 2 * k + g
                if tile == 0:
                    if ssm is not None and isinstance(i, int) and i == 0:
                        eng.wait_ge(s_sg, 2)
                    wait(eng, s_lo, 4 * Q + 4)
                    wait(eng, s_ac, 4 * (Q - 1))
                for c in range(NC):
                    h = high(hid[:, g, c, P * tile:P * tile + P])[:, 1::2]
                    hl = hlo[:, g, c, P * tile:P * tile + P]
                    at = DOWN + P * c
                    out = DB[g][:, tile, :]
                    eng.matmul(out, h, wh[:, k, at:at + P], start=c == 0, stop=False)
                    eng.matmul(out, h, wl[:, k, at:at + P], start=False, stop=False)
                    mm = eng.matmul(out, hl, wh[:, k, at:at + P], start=False, stop=c == NC - 1)
                if tile == 3:
                    mm.then_inc(s_dn, 1)

            def before(i, k, g):
                if g:
                    return i, k, 0
                if k:
                    return i, 0, 1
                return None if isinstance(i, int) and i == 0 else (i - 1, 1, 1)

            def expert(i, k):
                for g in range(2):
                    for c in range(NC):
                        unit(i, k, g, c)
                        if c == (1, 3)[layer] and (q := before(i, k, g)):
                            for tile in range(4):
                                down(*q, tile)
                    if ssm is not None and isinstance(i, int) and i + k + g == 0:
                        step_products()

            def end():
                for tile in range(4):
                    down(*((E // 2 - 1, 1, 1) if NE == E else (E // 2, 0, 1)), tile)

            def step_products():
                eng.wait_ge(s_xf, 3)
                for m in range(2):
                    eng.matmul(DB[m][:, :, :].rearrange("p a b -> p (a b)"), t["dtw"][:, :], xf[:, m * TG:m * TG + TG], start=True,
                               stop=True).then_inc(s_dtp, 1)
            each(eng, expert, end)

        @block.scalar
        def _(eng):
            def unit(i, k, g, c):
                U = 16 * i + 8 * k + 4 * g + c
                Q = 4 * i + 2 * k + g
                wait(eng, s_gu, U + 1)
                if layer == 0:
                    wait(eng, s_hid, U - 3)
                    eng.activation(act[:, c, :], FB[c % NF][:, :], ACT.Silu).then_inc(s_act, 1)
                else:
                    wait(eng, s_hid, U - 3)
                    eng.activation(act[:, c, :], FB[c % NF][:, :], ACT.Relu).then_inc(s_act, 1)
                    wait(eng, s_act, U + 1)
                    if c == 0:
                        wait(eng, s_dn, Q - 1)
                    eng.activation(hid[:, g, c, :], act[:, c, :], ACT.Square).then_inc(s_hid, 1)

            def state(i, d):
                n = 4 * i + d
                wait(eng, s_dt, 1)
                wait(eng, s_st, n - 1)
                eng.activation(ea[:, d % 2, :], dt[:, :], ACT.Exp, scale=t["A"][:, bass.ds(n, 1)]).then_inc(s_ea, 1)

            def expert(i, k):
                for g in range(2):
                    for c in range(NC):
                        unit(i, k, g, c)
                        if c == 1:
                            for d in states(i, k, g):
                                state(i, d)
                    if ssm is not None and isinstance(i, int) and i + k + g == 0:
                        for m in range(2):
                            eng.wait_ge(s_dtp, m + 1)
                            eng.activation(sg[:, m * TG:m * TG + TG], DB[m][:, :, :].rearrange("p a b -> p (a b)"),
                                           ACT.Sigmoid, bias=t["dtb"][:, 0:1]).then_inc(s_sg, 1)

            each(eng, expert)

        @block.vector
        def _(eng):
            def split(i, k):
                e = 2 * i + k
                wait(eng, s_w[k], 16 * i)
                wait(eng, s_dn, 2 * (e - 1))
                eng.tensor_copy(wh[:, k, :], wf[:, k, :]).then_inc(s_wh, 1)

            def unit(i, k, g, c):
                U = 16 * i + 8 * k + 4 * g + c
                Q = 4 * i + 2 * k + g
                h = hid[:, g, c, :]
                if layer == 0:
                    wait(eng, s_act, U + 1)
                    if c == 0:
                        wait(eng, s_dn, Q - 1)
                    eng.tensor_tensor(h, act[:, c, :], UB[c][:, :], ALU.mult).then_inc(s_hid, 1)
                    wait(eng, s_hid, U + 1)
                else:
                    wait(eng, s_hid, U + 1)
                eng.tensor_tensor(hlo[:, g, c, :], h, high(h)[:, 1::2], ALU.subtract).then_inc(s_lo, 1)

            def add(i, k, g):
                Q = 4 * i + 2 * k + g
                e = 2 * i + k
                wait(eng, s_dn, Q + 1)
                for tile in range(4):
                    xs = x[:, TB * b + 4 * g + tile, :]
                    eng.scalar_tensor_tensor(out=xs, in0=DB[g][:, tile, :],
                                             scalar=cw[:, TB * b + 4 * g + tile, bass.ds(e, 1)], in1=xs,
                                             op0=ALU.mult, op1=ALU.add).then_inc(s_ac, 1)

            def steps():
                eng.wait_ge(s_sg, 2)
                eng.tensor_scalar(dt[:, :], sg[:, :], 0.1 - 0.001, 0.001, ALU.mult, ALU.add).then_inc(s_dt, 1)
                eng.wait_ge(s_dt, 1)
                eng.tensor_tensor(us[:, :], dt[:, :], xf[:, :], ALU.mult).then_inc(s_us, 1)

            def scan(i, d):
                n = 4 * i + d
                wait(eng, s_bu, n + 1)
                wait(eng, s_ea, n + 1)
                wait(eng, s_y, n - 1)
                eng.tensor_tensor_scan(st[:, d % 2, :], ea[:, d % 2, :], bu[:, d % 2, :], 0.0, ALU.mult,
                                       ALU.add).then_inc(s_st, 1)

            def expert(i, k):
                for g in range(2):
                    for c in range(NC):
                        if c == 0 and g == 1:
                            if k == 0 and not (isinstance(i, int) and 2 * i + 1 >= NE):
                                split(i, 1)
                            elif k == 1 and not (isinstance(i, int) and 2 * i + 2 >= NE):
                                split(i + 1, 0)
                        unit(i, k, g, c)
                        if c == 1:
                            if q := expert_before(i, k, g):
                                add(*q)
                        if c == 2:
                            for d in states(i, k, g):
                                scan(i, d)
                    if ssm is not None and isinstance(i, int) and i + k + g == 0:
                        steps()

            def expert_before(i, k, g):
                if k:
                    return i, 0, g
                return None if isinstance(i, int) and i == 0 else (i - 1, 1, g)

            if ssm is not None:
                xs = xT[:, ssm * S:ssm * S + S]
                eng.tensor_scalar(xf[:, :], xs, t["cvw"][:, 1:2], t["cvb"][:, 0:1], ALU.mult, ALU.add).then_inc(s_xf, 1)
                eng.wait_ge(s_xf, 1)
                eng.scalar_tensor_tensor(out=xf[:, 1:S], in0=xs[:, 0:S - 1], scalar=t["cvw"][:, 0:1], in1=xf[:, 1:S],
                                         op0=ALU.mult, op1=ALU.add).then_inc(s_xf, 1)
                eng.wait_ge(s_xf, 2)
                eng.scalar_tensor_tensor(out=xf[:, 0:S - 1], in0=xs[:, 1:S], scalar=t["cvw"][:, 2:3],
                                         in1=xf[:, 0:S - 1], op0=ALU.mult, op1=ALU.add).then_inc(s_xf, 1)

            def last():
                for g in range(2):
                    add(*((E // 2 - 1, 1, g) if NE == E else (E // 2, 0, g)))

            each(eng, expert, last)

        @block.gpsimd
        def _(eng):
            def split(i, k):
                e = 2 * i + k
                wait(eng, s_wh, e)
                eng.tensor_tensor(wl[:, k, :], wf[:, k, :], wh[:, k, :], ALU.subtract).then_inc(s_wl, 1)

            def inputs(i, d):
                n = 4 * i + d
                wait(eng, s_us, 1)
                wait(eng, s_st, n - 1)
                eng.tensor_tensor(bu[:, d % 2, :], us[:, :], t["bc"][:, bass.ds(n, 1)].to_broadcast([P, S]),
                                  ALU.mult).then_inc(s_bu, 1)

            def sum_state(i, d):
                n = 4 * i + d
                wait(eng, s_st, n + 1)
                y = t["y"][:, ssm, :]
                if d == 0 and isinstance(i, int) and i == 0:
                    eng.tensor_copy(y, st[:, 0, :]).then_inc(s_y, 1)
                else:
                    wait(eng, s_y, n)
                    eng.tensor_tensor(y, y, st[:, d % 2, :], ALU.add).then_inc(s_y, 1)

            def expert(i, k):
                for g in range(2):
                    if g == 1:
                        if k == 0 and not (isinstance(i, int) and 2 * i + 1 >= NE):
                            split(i, 1)
                        elif k == 1 and not (isinstance(i, int) and 2 * i + 2 >= NE):
                            split(i + 1, 0)
                    for d in states(i, k, g):
                        inputs(i, d)
                        if d:
                            sum_state(i, d - 1)
                        elif not (isinstance(i, int) and i == 0):
                            sum_state(i - 1, 3)

            def last_sum():
                if ssm is not None:
                    sum_state(DS // 4 - 1, 3)

            each(eng, expert, last_sum)

    sem.end()


def program(nc, io, out):
    ctx = ExitStack()
    with ctx:
        def sb(name, shape, dt):
            return ctx.enter_context(nc.sbuf_tensor(name, shape, dt))

        t = {
            "x": sb("x", [P, NT, D], F32),
            "ident16": sb("ident16", [P, P], F16),
            "ident32": sb("ident32", [P, P], F32),
            "s_ident": ctx.enter_context(nc.semaphore("s_ident")),
        }
        with nc.sbuf_tensor("bout", [P, D], F32) as bout:
            attention(nc, ctx, io, t | {"bout": bout})
        t |= {
            "xT": sb("xT", [P, T], F32),
            "xl": sb("xl", [P, T], F16),
            "y": sb("y", [P, B, S], F32),
            "wf": sb("wf", [P, 2, 3 * FF], F32),
            "wh": sb("wh", [P, 2, 3 * FF], F16),
            "wl": sb("wl", [P, 2, 3 * FF], F16),
            "cw": sb("cw", [P, NT, E + 1], F32),
            "iota": sb("iota", [P, E], F32),
            "half": sb("half", [P, 1], F32),
            "gate": sb("gate", [P, E], F32),
            "router": sb("router", [P, E], F32),
            "dtw": sb("dtw", [P, D], F32),
            "dtb": sb("dtb", [P, 1], F32),
            "cvw": sb("cvw", [P, 3], F32),
            "cvb": sb("cvb", [P, 1], F32),
            "A": sb("A", [P, DS], F32),
            "bc": sb("bc", [P, DS], F32),
        }
        prepare_rest(nc, t, io)
        normalize_and_turn(nc, "n1", t, io, ((0, None, "gate", None), (1, None, "gate", None)), 0)
        experts(nc, "e1", t, io, 0, 0, None)
        normalize_and_turn(nc, "n2", t, io, ((0, None, None, None),), 0)
        experts(nc, "e2", t, io, 0, 1, 0)
        normalize_and_turn(nc, "n3", t, io, ((0, "y", "router", None), (1, None, None, None)), 1)
        experts(nc, "e3", t, io, 1, 0, 1)
        normalize_and_turn(nc, "n4", t, io, ((1, "y", "router", None), (0, None, None, out[0])), 1)
        experts(nc, "e4", t, io, 1, 1, None)
        normalize_and_turn(nc, "n5", t, io, ((1, None, None, out[1]),))


def layout(inputs):
    import numpy as np
    a = {k: np.asarray(v) for k, v in inputs.items()}
    x = a["L0_attn_x"].reshape(T, D)
    wq = a["L0_attn_w_q"].reshape(D, H, DH)
    wkv = a["L0_attn_w_kv"].reshape(D, 2, H, DH)

    def up(w):
        return w.transpose(2, 0, 1)

    def down(w):
        return w.reshape(-1, D, NC, P).transpose(3, 0, 2, 1).reshape(P, -1, NC * D)

    w_fc = np.concatenate([a["L1_ffn_w_fc"], a["L1_ffn_shared_fc"][None]])
    w_proj = np.concatenate([a["L1_ffn_w_proj"], a["L1_ffn_shared_proj"][None]])
    named = {
        "x": x,
        "xT": x.T,
        "wqkv": np.concatenate([wq, wkv[:, 0], wkv[:, 1]], axis=2).reshape(D, H * QKV),
        "wout": a["L0_attn_w_out"].reshape(H // 2, P, D).transpose(1, 0, 2).reshape(P, H // 2 * D),
        "b_out": a["L0_attn_b_out"],
        "scale": a["L0_attn_scale"].reshape(H),
        "w0": np.concatenate([up(a["L0_ffn_wg"]), up(a["L0_ffn_wu"]), down(a["L0_ffn_wd"])], axis=2).reshape(P, -1),
        "w1": np.concatenate([up(w_fc), down(w_proj)], axis=2).reshape(P, -1),
        "gateT": a["L0_ffn_gate_w"].T,
        "routerT": a["L1_ffn_router_w"].T,
        "a_log": a["L1_attn_a_log"],
        "b": a["L1_attn_b"],
        "c": a["L1_attn_c"],
        "dtwT": a["L1_attn_dt_w"].T,
        "dt_b": a["L1_attn_dt_b"].reshape(D, 1),
        "conv_w": a["L1_attn_conv_w"].reshape(D, 3),
        "conv_b": a["L1_attn_conv_b"].reshape(D, 1),
    }
    return {k: np.ascontiguousarray(v) for k, v in named.items()}


def kernel(**inputs):
    import numpy as np
    import concourse.bacc as bacc
    from concourse.bass_utils import run_bass_kernel_spmd as run

    nc = bacc.Bacc("TRN2", target_bir_lowering=False, num_devices=1)
    arrays = {f"in_{k}": v for k, v in layout(inputs).items()}
    io = {k[3:]: nc.dram_tensor(k, a.shape, mybir.dt.from_np(a.dtype), kind="ExternalInput").ap()
          for k, a in arrays.items()}
    out = nc.dram_tensor("out", (B, S, D), F32, kind="ExternalOutput").ap()
    program(nc, io, out)
    return run(nc, [arrays], core_ids=[0]).results[0]["out"]
```

```python
import concourse.bass as bass
from concourse import mybir
from contextlib import ExitStack

F32 = mybir.dt.float32
F16 = mybir.dt.float16
BF16 = mybir.dt.bfloat16
U32 = mybir.dt.uint32
ALU = mybir.AluOpType
ACT = mybir.ActivationFunctionType
AX = mybir.AxisListType.X

P = 128
B, S, D = 2, 1024, 128
T = B * S
NT = T // P
H, DH = 16, 64
QKV = 3 * DH
E = 8
FF = 512
NC = FF // P
DS = 16
EPS = 1e-5


def high(ap):
    return ap.bitcast(BF16)


def wait(eng, sem, count):
    if not isinstance(count, int) or count > 0:
        eng.wait_ge(sem, count)


SLOTS = 16
QW = 256
KT = 4
PB = 4
LAG = 2
PJ = 8
VW = 130
STK = 5 * DH
WCH = 4
TAIL = 32
RESIDUAL_AT = 14

POOL_LO = (9, 13)
GROUP_AT = (0, 3, 5, 7)
SUM_AT = (1, 4, 6, 10)
NORM_AT = (3, 6, 9, 11)
TURN_AT = (6, 7, 9, 10, 11, 12, 13, 14)
OUT_TURN_AT = (31, 32, 33, 34, 35, 36, 37, 40)
OUT_AT = (42, 43, 45, 46, 58, 59, 61, 63)


def low_count(i, s, pool):
    mine = [k for k in range(SLOTS) if (k in POOL_LO) == pool]
    return 2 * len(mine) * i + s // SLOTS * len(mine) + sum(k <= s % SLOTS for k in mine)


def proj_slot(j):
    return GROUP_AT[j // 2] + j % 2


def tp_slot(j):
    return TURN_AT[j]


def at_slot(place, s, n=PJ):
    return next((j for j in range(n) if place(j) == s), None)


def before(place, s, n=PJ):
    return sum(place(j) < s for j in range(n))


def turn_slot(u):
    return OUT_TURN_AT[u]


def out_slot(u):
    return OUT_AT[u]


def out_unit(s, place):
    for back in (0, 1):
        if (u := at_slot(place, s + 2 * SLOTS * back)) is not None:
            return back, u
    return None


def out_before(s, place):
    return before(place, s) + before(place, s + 2 * SLOTS) - PJ


class Semaphores:

    def __init__(self, nc, tag):
        self.nc, self.tag, self.made = nc, tag, []

    def __call__(self, name):
        self.made.append(self.nc.alloc_semaphore(name=f"{name}_{self.tag}"))
        return self.made[-1]

    def end(self):
        self.nc.clear_and_free_semaphores(self.made)
        self.nc.all_engine_barrier()


class Constants:

    def __init__(self, nc, t, io, sb, sem):
        self.t, self.io = t, io
        self.al, self.ab, self.na, self.en, self.ln, self.mxa, self.bb, self.cc = (
            sb("c_" + n, [P, DS], F32) for n in ("al", "ab", "na", "en", "ln", "mxa", "bb", "cc"))
        self.int_iota = sb("int_iota", [P, E], mybir.dt.int32)
        self.s_loaded, self.s_weights, self.s_high, self.s_low, self.s_made, self.s_sum, self.s_exp = (
            sem(n) for n in ("c_loaded", "c_weights", "c_high", "c_low", "c_made", "c_sum", "c_exp"))

    def sync(self, eng):
        t, io = self.t, self.io
        loads = ((self.al[:, :], "a_log"), (self.bb[:, :], "b"), (self.cc[:, :], "c"), (t["dtw"][:, :], "dtwT"),
                 (t["dtb"][:, :], "dt_b"), (t["cvw"][:, :], "conv_w"), (t["cvb"][:, :], "conv_b"),
                 (t["gate"][:, :], "gateT"), (t["router"][:, :], "routerT"))
        for dst, name in loads:
            eng.dma_start(dst, io[name]).then_inc(self.s_loaded, 16)
        eng.dma_start(t["wf"][:, :, :], io["w0"][:, 0:2 * 3 * FF].rearrange("p (k w) -> p k w", k=2)).then_inc(
            self.s_weights, 16)
        eng.wait_ge(self.s_loaded, 16 * len(loads))
        eng.wait_ge(self.s_weights, 16)

    def gpsimd(self, eng):
        t = self.t
        eng.iota(self.int_iota[:, :], pattern=[[1, E]], base=0, channel_multiplier=0).then_inc(self.s_made, 1)
        eng.memset(t["cw"][:, :, E:E + 1], 1.0).then_inc(self.s_made, 1)
        eng.wait_ge(self.s_made, 2)
        eng.tensor_copy(t["iota"][:, :], self.int_iota[:, :]).then_inc(self.s_made, 1)
        eng.wait_ge(self.s_high, 1)
        eng.tensor_tensor(t["wl"][:, 0, :], t["wf"][:, 0, :], t["wh"][:, 0, :], ALU.subtract).then_inc(self.s_low, 1)

    def vector(self, eng):
        t, s_sum = self.t, self.s_sum
        eng.wait_ge(self.s_weights, 16)
        eng.tensor_copy(t["wh"][:, 0, :], t["wf"][:, 0, :]).then_inc(self.s_high, 1)
        eng.wait_ge(self.s_loaded, 16 * 9)
        eng.tensor_scalar(self.na[:, :], self.al[:, :], -1.0, None, ALU.mult).then_inc(s_sum, 1)
        eng.tensor_tensor(t["bc"][:, :], self.bb[:, :], self.cc[:, :], ALU.mult).then_inc(s_sum, 1)
        eng.tensor_scalar(self.mxa[:, :], self.al[:, :], 0.0, None, ALU.max).then_inc(s_sum, 1)
        eng.wait_ge(s_sum, 3)
        eng.tensor_tensor(self.ab[:, :], self.al[:, :], self.na[:, :], ALU.min).then_inc(s_sum, 1)
        eng.wait_ge(self.s_exp, 2)
        eng.tensor_tensor(self.na[:, :], self.mxa[:, :], self.ln[:, :], ALU.add).then_inc(s_sum, 1)
        eng.wait_ge(s_sum, 5)
        eng.tensor_scalar(t["A"][:, :], self.na[:, :], -1.0, None, ALU.mult).then_inc(s_sum, 1)

    def scalar(self, eng):
        eng.wait_ge(self.s_sum, 4)
        eng.activation(self.en[:, :], self.ab[:, :], ACT.Exp).then_inc(self.s_exp, 1)
        eng.wait_ge(self.s_exp, 1)
        eng.activation(self.ln[:, :], self.en[:, :], ACT.Ln, bias=1.0).then_inc(self.s_exp, 1)


def attention(nc, io, t):
    es = ExitStack()
    sem = Semaphores(nc, "at")

    def sb(name, shape, dt):
        return es.enter_context(nc.sbuf_tensor(name, shape, dt))

    def ps(name, shape, dt):
        return es.enter_context(nc.psum_tensor(name, shape, dt))

    with es:
        w_hi = sb("w_hi", [P, H * QKV], F16)
        w_lo = sb("w_lo", [P, H * QKV], F16)
        xT_hi = sb("xT_hi", [P, T], F16)
        xT_lo = sb("xT_lo", [P, T], F16)
        wo = sb("wo", [P, H // 2 * D], F32)
        esc = sb("esc", [P, H], F32)
        scl = sb("scl", [P, H], F32)
        cur_esc = sb("cur_esc", [P, 2], F32)
        cur_nesc = sb("cur_nesc", [P, 2], F32)
        raw = sb("raw", [P, 4, 4, QKV], F32)
        sq = sb("sq", [P, 2, 4, 2, DH], F32)
        ss = sb("ss", [P, 2, 4, 2], F32)
        rn = sb("rn", [P, 2, 4, 2], F32)
        nrm = sb("nrm", [P, 2, 4, 2, DH], F32)
        stk = sb("stk", [P, 4, 4, STK], F16)
        QK = sb("QK", [P, 2, 3, T], F16)
        V = sb("V", [P, 2, NT, VW], F16)
        Pr = sb("Pr", [P, PB, KT, QW], F32)
        Pl = sb("Pl", [P, PB, KT, QW], F16)
        rden = sb("rden", [P, 4, 2], F32)
        Or = sb("Or", [P, 4, 258], F32)
        osum = sb("osum", [P, 2, 2, DH], F32)
        Ob = sb("Ob", [P, NT, 2 * DH], F32)
        OT = sb("OT", [P, PJ, 2, P], F32)
        half = t["half"]
        bout = sb("bout", [P, D], F32)
        w_f32 = QK[:, 1, :, :].rearrange("p k t -> p (k t)").bitcast(F32)
        xT_f32 = Pr[:, 0:2, :, :].rearrange("p a b c -> p (a b c)")
        ss2 = sb("ss2", [P, 2, 4, 2], F32)

        SC = [ps(f"SC{i}", [P, KT, QW], F32) for i in range(2)]
        OP = [ps(f"OP{i}", [P, 512], F32) for i in range(2)]
        M0 = ps("M0", [P, 512], F32)
        M1 = ps("M1", [P, 512], F32)

        s_loaded = {k: sem("s_ld_" + k) for k in ("x", "wo", "scl")}
        s_w_loaded = [sem(f"s_w_loaded{c}") for c in range(WCH)]
        s_x_loaded = [sem(f"s_x_loaded{m}") for m in range(2)]
        s_ones = sem("s_ones")
        s_w_high = sem("s_w_high")
        s_w_low = sem("s_w_low")
        s_x_high = sem("s_x_high")
        s_x_low = sem("s_x_low")
        s_scales = sem("s_scales")
        s_head_scale = sem("s_head_scale")
        s_scores = sem("s_scores")
        s_exps = sem("s_exps")
        s_low_probs = sem("s_low_probs")
        s_low_probs_pool = sem("s_low_probs_pool")
        s_av_products = sem("s_av_products")
        s_av_read = sem("s_av_read")
        s_inverse_sums = sem("s_inverse_sums")
        s_projected = sem("s_projected")
        s_raw_read = sem("s_raw_read")
        s_squares = sem("s_squares")
        s_square_sums = sem("s_square_sums")
        s_clamped = sem("s_clamped")
        s_powers = sem("s_powers")
        s_inverse_norms = sem("s_inverse_norms")
        s_normalized = sem("s_normalized")
        s_v_high = sem("s_v_high")
        s_v_low = sem("s_v_low")
        s_qk_high = sem("s_qk_high")
        s_k_copied = sem("s_k_copied")
        s_qk_low = sem("s_qk_low")
        s_turned = sem("s_turned")
        s_outputs = sem("s_outputs")
        s_output_sums = sem("s_output_sums")
        s_out_turned = sem("s_out_turned")
        s_out_turned_read = sem("s_out_turned_read")
        s_out_product = sem("s_out_product")
        s_out_added = sem("s_out_added")
        s_residual = sem("s_residual")
        s_half = sem("s_half")
        s_ident = sem("s_ident")
        s_turned_read_vector = sem("s_turned_read_vector")
        s_turned_read_scalar = sem("s_turned_read_scalar")
        constants = Constants(nc, t, io, sb, sem)
        block = es.enter_context(nc.Block())

        def heads(eng, emit, constants=None):
            for s in range(2 * SLOTS):
                emit(0, s)
            with eng.Fori(1, H // 2 - 1) as i:
                for s in range(2 * SLOTS):
                    emit(i, s)
            for s in range(2 * SLOTS):
                emit(H // 2 - 1, s)
            for s in range(TAIL):
                emit(H // 2, s)
                if s == SLOTS // 2 and constants:
                    constants(eng)

        def projection_bank(h, j):
            return OP[0] if isinstance(h, int) and h == 0 and j % 2 else M0

        def chunk(c):
            return slice(c * H * QKV // WCH, (c + 1) * H * QKV // WCH)

        def out_bank(i, u):
            return SC[0][:, 0, :] if isinstance(i, int) and i == H // 2 - 1 and u % 2 else M0[:, 0:2 * P]

        def ended(i):
            return isinstance(i, int) and i == H // 2

        def prepares(i, s):
            return not (isinstance(i, int) and 2 * i + s // SLOTS >= H - 1)

        def started(i, back):
            return not (isinstance(i, int) and i - back < 0)

        def exists(i, back):
            return started(i, back) and not (ended(i) and not back)

        @block.sync
        def _(eng):
            for c in range(WCH):
                eng.dma_start(w_f32[:, chunk(c)], io["wqkv"][:, chunk(c)]).then_inc(s_w_loaded[c], 16)
                if c == 0:
                    for m in range(2):
                        cs = slice(S * m, S * m + S)
                        eng.dma_start(xT_f32[:, cs], io["xT"][:, cs]).then_inc(s_x_loaded[m], 16)
                    eng.dma_start(scl[:, :], io["scale"].partition_broadcast(P)).then_inc(s_loaded["scl"], 16)
            eng.dma_start(wo[:, :], io["wout"]).then_inc(s_loaded["wo"], 16)
            eng.dma_start(t["x"][:, :, :], io["x"].rearrange("(t p) d -> p t d", p=P)).then_inc(s_loaded["x"], 16)
            eng.dma_start(bout[:, :], io["b_out"].partition_broadcast(P)).then_inc(s_loaded["x"], 16)
            constants.sync(eng)

        @block.tensor
        def _(eng):
            ident16, ident32 = t["ident16"], t["ident32"]

            def m0_free(h, j, i, s):
                wait(eng, s_squares, 8 * h + j)
                wait(eng, s_out_added, 8 * i + out_before(s, out_slot))

            def m1_free(h, j, i, s):
                wait(eng, s_turned_read_vector, 4 * h + (j + 1) // 2)
                wait(eng, s_turned_read_scalar, 4 * h + j // 2)
                wait(eng, s_out_turned_read, 8 * i + out_before(s, turn_slot))

            def proj(h, j):
                for r in range(2):
                    tile = 2 * j + r
                    out = projection_bank(h, j)[:, QKV * r:QKV * r + QKV]
                    hi, lo = xT_hi[:, P * tile:P * tile + P], xT_lo[:, P * tile:P * tile + P]
                    wh, wl = w_hi[:, bass.ds(QKV * h, QKV)], w_lo[:, bass.ds(QKV * h, QKV)]
                    eng.matmul(out, hi, wh, start=True, stop=False)
                    eng.matmul(out, hi, wl, start=False, stop=False)
                    mm = eng.matmul(out, lo, wh, start=False, stop=True)
                mm.then_inc(s_projected, 1)

            def transposes(h, j):
                g = j // 2
                wait(eng, s_qk_high, 4 * h + g + 1)
                wait(eng, s_k_copied, 4 * h + g + 1)
                wait(eng, s_qk_low, 4 * h + g + 1)
                m1 = M1[:, :].bitcast(F16)
                for kind in range(3):
                    at = (0, 2 * DH, 3 * DH)[kind]
                    for r in range(2):
                        mm = eng.transpose(m1[:, (2 * kind + r) * P:(2 * kind + r + 1) * P],
                                           stk[:, g, 2 * (j % 2) + r, at:at + P], ident16[:, :])
                mm.then_inc(s_turned, 1)

            def scores(i, s):
                n, h, b = 32 * i + s, 2 * i + s // SLOTS, s // SLOTS
                s %= SLOTS
                bat, q, kh = s // 8, s % 8 // 2, s % 2
                if s == 0:
                    wait(eng, s_turned_read_vector, 4 * h + 4)
                    wait(eng, s_turned_read_scalar, 4 * h + 4)
                wait(eng, s_exps, n - 1)
                for kt in range(KT):
                    key = bat * S + (kh * KT + kt) * P
                    rhs = QK[:, b, 0, bat * S + q * QW:bat * S + q * QW + QW]
                    out = SC[s % 2][:, kt, :]
                    eng.matmul(out, QK[:, b, 1, key:key + P], rhs, start=True, stop=False)
                    mm = eng.matmul(out, QK[:, b, 2, key:key + P], rhs, start=False, stop=True)
                mm.then_inc(s_scores, 1)

            def av(i, s):
                n, h, b = 32 * i + s, 2 * i + s // SLOTS, s // SLOTS
                s %= SLOTS
                bat, kh, u = s // 8, s % 2, s // 2
                pool = s in POOL_LO
                wait(eng, s_low_probs_pool if pool else s_low_probs, low_count(i, s + SLOTS * b, pool))
                if s == 0:
                    wait(eng, s_v_high, 4 * h + 4)
                    wait(eng, s_v_low, 4 * h + 4)
                if kh == 0:
                    wait(eng, s_av_read, 16 * i + 8 * b + u - 1)
                for kt in range(KT):
                    tile = bat * 8 + kh * KT + kt
                    for r in range(2):
                        hi = high(Pr[:, s % PB, kt, P * r:P * r + P])[:, 1::2]
                        lo = Pl[:, s % PB, kt, P * r:P * r + P]
                        at = 129 * r
                        first = kh == 0 and kt == 0 and r == 0
                        last = kh == 1 and kt == KT - 1 and r == 1
                        eng.matmul(OP[u % 2][:, at:at + 129], hi, V[:, b, tile, 0:129],
                                   start=first, stop=False, skip_group_check=True)
                        mm = eng.matmul(OP[u % 2][:, at:at + 65], lo, V[:, b, tile, 0:65],
                                        start=False, stop=last, skip_group_check=True)
                mm.then_inc(s_av_products, 1)

            def out_transposes(i, u):
                wait(eng, s_outputs, 16 * i + 8 + u + 1)
                for r in range(2):
                    mm = eng.transpose(M1[:, P * r:P * r + P], Ob[:, 2 * u + r, :], ident32[:, :])
                mm.then_inc(s_out_turned, 1)

            def out_product(i, u):
                wait(eng, s_out_turned_read, 8 * i + u + 1)
                for r in range(2):
                    mm = eng.matmul(out_bank(i, u)[:, P * r:P * r + P], OT[:, u, r, :],
                                    wo[:, bass.ds(D * i, D)], start=True, stop=True)
                mm.then_inc(s_out_product, 1)

            def slot(i, s):
                h, sh = 2 * i + s // SLOTS, s % SLOTS
                pj, tp = before(proj_slot, sh), before(tp_slot, sh)
                if not prepares(i, s):
                    pj, tp = (0, 0) if ended(i) or s >= SLOTS else (pj, tp)
                nh = H if not prepares(i, s) else h + 1
                if isinstance(i, int) and i == 0 and s == SLOTS:
                    eng.wait_ge(s_w_low, WCH)
                if not ended(i):
                    scores(i, s)
                if s >= LAG and not ended(i):
                    av(i, s - LAG)
                elif s < LAG and started(i, 1):
                    av(i - 1, s + 2 * SLOTS - LAG)
                if (x := out_unit(s, turn_slot)) and exists(i, x[0]):
                    m1_free(nh, tp, i, s)
                    out_transposes(i - x[0], x[1])
                if (x := out_unit(s, out_slot)) and exists(i, x[0]):
                    if ended(i):
                        wait(eng, s_exps, 2 * SLOTS * (H // 2))
                        wait(eng, s_out_added, 8 * i + out_before(s, out_slot) - 1)
                    else:
                        m0_free(nh, pj, i, s)
                    out_product(i - x[0], x[1])
                if prepares(i, s):
                    if (j := at_slot(proj_slot, sh)) is not None:
                        m0_free(h + 1, j, i, s)
                        proj(h + 1, j)
                    if (j := at_slot(tp_slot, sh)) is not None:
                        m1_free(h + 1, j, i, s)
                        transposes(h + 1, j)

            eng.wait_ge(s_w_low, 1)
            eng.wait_ge(s_ident, 4)
            for j in range(PJ):
                eng.wait_ge(s_x_low, j // (PJ // 2) + 1)
                wait(eng, s_squares, j - 1)
                proj(0, j)
            for j in range(PJ):
                m1_free(0, j, 0, 0)
                transposes(0, j)
            eng.wait_ge(s_loaded["wo"], 16)
            eng.wait_ge(s_squares, PJ)
            heads(eng, slot)

        @block.scalar
        def _(eng):
            def read_proj(h, hb, j):
                J, G, g, b = 8 * h + j, 4 * h + j // 2, j // 2, j // 2 % 2
                r = 2 * (j % 2)
                wait(eng, s_projected, J + 1)
                if j % 2 == 0:
                    wait(eng, s_normalized, G - 3)
                    wait(eng, s_v_low, G - 3)
                    wait(eng, s_square_sums, G - 1)
                m0 = projection_bank(h, j)[:, 0:2 * QKV].rearrange("p (r c) -> p r c", r=2)
                eng.activation(raw[:, g, r:r + 2, :], m0, ACT.Copy).then_inc(s_raw_read, 1)
                eng.activation(sq[:, b, r:r + 2, :, :], m0[:, :, 0:2 * DH].rearrange("p r (k d) -> p r k d", k=2),
                               ACT.Square).then_inc(s_squares, 1)

            def high_values(h, hb, g):
                wait(eng, s_raw_read, 8 * h + 2 * g + 2)
                wait(eng, s_av_products, SLOTS * (h - 1))
                eng.activation(V[:, hb, 4 * g:4 * g + 4, 0:DH], raw[:, g, :, 2 * DH:QKV], ACT.Copy).then_inc(
                    s_v_high, 1)

            def read_transposes(h, hb, j):
                wait(eng, s_turned, 8 * h + j + 1)
                eng.activation(QK[:, hb, :, 2 * P * j:2 * P * j + 2 * P],
                               M1[:, :].bitcast(F16)[:, 0:6 * P].rearrange("p (k c) -> p k c", k=3),
                               ACT.Copy).then_inc(s_turned_read_scalar, 1)

            def read_out_transposes(i, u):
                wait(eng, s_out_turned, 8 * i + u + 1)
                eng.activation(OT[:, u, :, :], M1[:, 0:2 * P].rearrange("p (r c) -> p r c", r=2), ACT.Copy).then_inc(
                    s_out_turned_read, 1)

            def read_out(i, s):
                b, u = s // SLOTS, s % SLOTS // 2
                m = 16 * i + 8 * b + u
                wait(eng, s_av_products, 2 * m + 2)
                wait(eng, s_outputs, m - 3)
                eng.activation(Or[:, u % 4, :], OP[u % 2][:, 0:258], ACT.Copy).then_inc(s_av_read, 1)

            def exps(i, s):
                n, b = 32 * i + s, s // SLOTS
                if s % SLOTS == 0:
                    wait(eng, s_head_scale, 4 * i + 2 * b + 2)
                wait(eng, s_scores, n + 1)
                wait(eng, s_av_products, n - PB + 1)
                eng.activation(Pr[:, s % PB, :, :], SC[s % 2][:, :, :], ACT.Exp,
                               bias=cur_nesc[:, b:b + 1]).then_inc(s_exps, 1)

            def slot(i, s):
                h, sh = 2 * i + s // SLOTS, s % SLOTS
                if isinstance(i, int) and i == 0 and s == TURN_AT[0]:
                    eng.wait_ge(s_w_low, WCH)
                if not ended(i):
                    exps(i, s)
                if (x := out_unit(s, turn_slot)) and exists(i, x[0]):
                    read_out_transposes(i - x[0], x[1])
                if s % 2 == 0:
                    if s >= 4 and not ended(i):
                        read_out(i, s - 4)
                    elif s < 4 and started(i, 1):
                        read_out(i - 1, s + 2 * SLOTS - 4)
                if prepares(i, s):
                    prepare(h + 1, (s // SLOTS + 1) % 2, sh)

            def prepare(h, hb, s):
                if (j := at_slot(proj_slot, s)) is not None:
                    read_proj(h, hb, j)
                if (g := at_slot(SUM_AT.__getitem__, s, 4)) is not None:
                    high_values(h, hb, g)
                if (j := at_slot(tp_slot, s)) is not None and j % 2:
                    read_transposes(h, hb, j)

            for m in range(2):
                cs = slice(S * m, S * m + S)
                eng.wait_ge(s_x_loaded[m], 16)
                eng.activation(xT_hi[:, cs], xT_f32[:, cs], ACT.Copy).then_inc(s_x_high, 1)
            eng.wait_ge(s_loaded["scl"], 16)
            eng.activation(esc[:, :], scl[:, :], ACT.Exp).then_inc(s_scales, 1)
            for j in range(PJ):
                read_proj(0, 0, j)
                if j % 2:
                    high_values(0, 0, j // 2)
            for c in range(1, WCH):
                eng.wait_ge(s_w_loaded[c], 16)
                eng.activation(w_hi[:, chunk(c)], w_f32[:, chunk(c)], ACT.Copy).then_inc(s_w_high, 1)
            for j in range(1, PJ, 2):
                read_transposes(0, 0, j)
            eng.wait_ge(s_x_low, 2)
            heads(eng, slot, constants.scalar)

        @block.vector
        def _(eng):
            def square_sums(h, hb, g):
                G, b = 4 * h + g, g % 2
                wait(eng, s_squares, 8 * h + 2 * g + 2)
                eng.tensor_reduce(ss[:, b, :, :], sq[:, b, :, :, :], AX, ALU.add).then_inc(s_square_sums, 1)
                wait(eng, s_square_sums, G + 1)
                wait(eng, s_powers, G - 1)
                eng.tensor_scalar(ss2[:, b, :, :], ss[:, b, :, :], 1e-24, None, ALU.max).then_inc(s_clamped, 1)

            def normalize(h, hb, g):
                G, b = 4 * h + g, g % 2
                wait(eng, s_inverse_norms, G + 1)
                wait(eng, s_raw_read, 8 * h + 2 * g + 2)
                wait(eng, s_qk_high, G - 1)
                wait(eng, s_qk_low, G - 1)
                qk = raw[:, g, :, 0:2 * DH].rearrange("p t (k d) -> p t k d", k=2)
                eng.tensor_tensor(nrm[:, b, :, :, :], qk, rn[:, b, :, :].unsqueeze(3).to_broadcast([P, 4, 2, DH]),
                                  ALU.mult).then_inc(s_normalized, 1)

            def high_parts(h, hb, g):
                G, b = 4 * h + g, g % 2
                wait(eng, s_normalized, G + 1)
                wait(eng, s_turned, 8 * (h - 1) + 2 * g + 2)
                out = stk[:, g, :, 0:4 * DH].rearrange("p t (k x) -> p t k x", k=2)[:, :, :, 0:DH]
                eng.tensor_copy(out, nrm[:, b, :, :, :]).then_inc(s_qk_high, 1)

            def copy_keys(h, hb, g):
                G, b = 4 * h + g, g % 2
                wait(eng, s_qk_high, G + 1)
                eng.tensor_copy(stk[:, g, :, 4 * DH:5 * DH], stk[:, g, :, 2 * DH:3 * DH]).then_inc(s_k_copied, 1)

            def read_transposes(h, hb, j):
                wait(eng, s_turned, 8 * h + j + 1)
                eng.tensor_copy(QK[:, hb, :, 2 * P * j:2 * P * j + 2 * P].bitcast(U32),
                                M1[:, 0:3 * P].bitcast(U32).rearrange("p (k c) -> p k c", k=3)).then_inc(
                                    s_turned_read_vector, 1)

            def low_probs(i, s):
                n = 32 * i + s
                wait(eng, s_exps, n + 1)
                wait(eng, s_av_products, n - PB + 1)
                pr = Pr[:, s % PB, :, :].rearrange("p a b -> p (a b)")
                eng.tensor_tensor(Pl[:, s % PB, :, :].rearrange("p a b -> p (a b)"), pr, high(pr)[:, 1::2],
                                  ALU.subtract).then_inc(s_low_probs, 1)

            def low_weights(c):
                eng.wait_ge(s_w_high, c + 1)
                eng.tensor_tensor(w_lo[:, chunk(c)], w_f32[:, chunk(c)], w_hi[:, chunk(c)],
                                  ALU.subtract).then_inc(s_w_low, 1)

            def start_residual():
                eng.wait_ge(s_loaded["x"], 32)
                eng.tensor_tensor(t["x"][:, :, :], t["x"][:, :, :],
                                  bout[:, :].unsqueeze(1).to_broadcast([P, NT, D]), ALU.add).then_inc(s_residual, 1)

            def inverse_sums(i, s):
                b, u = s // SLOTS, s % SLOTS // 2
                m = 16 * i + 8 * b + u
                wait(eng, s_av_read, m + 1)
                wait(eng, s_outputs, m - 3)
                eng.reciprocal(rden[:, u % 4, :], Or[:, u % 4, DH:DH + 130:129]).then_inc(s_inverse_sums, 1)

            def add_out(i, u):
                wait(eng, s_out_product, 8 * i + u + 1)
                acc = t["x"][:, 2 * u:2 * u + 2, :]
                eng.tensor_tensor(acc, acc, out_bank(i, u).rearrange("p (r c) -> p r c", r=2),
                                  ALU.add).then_inc(s_out_added, 1)

            def head_scale(b, h):
                wait(eng, s_inverse_norms, 4 * (h - 1))
                wait(eng, s_exps, SLOTS * (h - 1))
                eng.tensor_copy(cur_esc[:, b:b + 1], esc[:, bass.ds(h, 1)]).then_inc(s_head_scale, 1)
                eng.tensor_scalar(cur_nesc[:, b:b + 1], esc[:, bass.ds(h, 1)], -1.0, None, ALU.mult).then_inc(
                    s_head_scale, 1)

            def prepare(h, hb, s):
                if (j := at_slot(tp_slot, s)) is not None and j % 2 == 0:
                    read_transposes(h, hb, j)
                if s == 0:
                    head_scale(hb, h)
                if (g := at_slot(SUM_AT.__getitem__, s, 4)) is not None:
                    square_sums(h, hb, g)
                if (g := at_slot(NORM_AT.__getitem__, s, 4)) is not None:
                    normalize(h, hb, g)
                    high_parts(h, hb, g)
                    copy_keys(h, hb, g)

            def slot(i, s):
                h, sh = 2 * i + s // SLOTS, s % SLOTS
                if not ended(i) and sh not in POOL_LO:
                    low_probs(i, s)
                if isinstance(i, int) and i == 0:
                    if s == RESIDUAL_AT:
                        start_residual()
                if (x := out_unit(s, out_slot)) and exists(i, x[0]):
                    if isinstance(i, int) and i < 2:
                        eng.wait_ge(s_residual, 1)
                    add_out(i - x[0], x[1])
                if prepares(i, s):
                    prepare(h + 1, (s // SLOTS + 1) % 2, sh)
                if s % 2 == 0:
                    if s >= 4 and not ended(i):
                        inverse_sums(i, s - 4)
                    elif s < 4 and started(i, 1):
                        inverse_sums(i - 1, s + 2 * SLOTS - 4)


            eng.memset(V[:, :, :, DH:DH + 1], 1.0).then_inc(s_ones, 1)
            eng.wait_ge(s_w_loaded[0], 16)
            eng.tensor_copy(w_hi[:, chunk(0)], w_f32[:, chunk(0)]).then_inc(s_w_high, 1)
            low_weights(0)
            for m in range(2):
                cs = slice(S * m, S * m + S)
                eng.wait_ge(s_x_high, m + 1)
                eng.tensor_tensor(xT_lo[:, cs], xT_f32[:, cs], xT_hi[:, cs], ALU.subtract).then_inc(s_x_low, 1)
            eng.wait_ge(s_scales, 1)
            head_scale(0, 0)
            square_sums(0, 0, 0)
            for g in range(4):
                if g < 3:
                    square_sums(0, 0, g + 1)
                normalize(0, 0, g)
                high_parts(0, 0, g)
                copy_keys(0, 0, g)
                if g:
                    low_weights(g)
                    read_transposes(0, 0, 2 * (g - 1))
            read_transposes(0, 0, 6)
            heads(eng, slot, constants.vector)

        @block.gpsimd
        def _(eng):
            def low_probs(i, s):
                n = 32 * i + s
                wait(eng, s_exps, n + 1)
                wait(eng, s_av_products, n - PB + 1)
                pr = Pr[:, s % PB, :, :].rearrange("p a b -> p (a b)")
                eng.tensor_tensor(Pl[:, s % PB, :, :].rearrange("p a b -> p (a b)"), pr, high(pr)[:, 1::2],
                                  ALU.subtract).then_inc(s_low_probs_pool, 1)

            def divide(i, s):
                b, u = s // SLOTS, s % SLOTS // 2
                m = 16 * i + 8 * b + u
                wait(eng, s_av_read, m + 1)
                o = Or[:, u % 4, :].rearrange("p (r c) -> p r c", r=2)
                eng.tensor_tensor(osum[:, u % 2, :, :], o[:, :, 0:DH], o[:, :, DH + 1:], ALU.add).then_inc(
                    s_output_sums, 1)
                wait(eng, s_output_sums, m + 1)
                wait(eng, s_inverse_sums, m + 1)
                eng.tensor_tensor(Ob[:, 2 * u:2 * u + 2, DH * b:DH * b + DH], osum[:, u % 2, :, :],
                                  rden[:, u % 4, :].unsqueeze(2).to_broadcast([P, 2, DH]), ALU.mult).then_inc(
                                      s_outputs, 1)

            def inverse_norms(h, hb, g):
                G, b = 4 * h + g, g % 2
                wait(eng, s_clamped, G + 1)
                wait(eng, s_normalized, G - 1)
                eng.tensor_tensor(rn[:, b, :, :], ss2[:, b, :, :],
                                  half[:, 0:1].unsqueeze(2).to_broadcast([P, 4, 2]), ALU.pow).then_inc(s_powers, 1)
                wait(eng, s_powers, G + 1)
                wait(eng, s_head_scale, 2 * h + 1)
                eng.tensor_tensor(rn[:, b, :, 0], rn[:, b, :, 0],
                                  cur_esc[:, hb:hb + 1].to_broadcast([P, 4]), ALU.mult).then_inc(s_inverse_norms, 1)

            def low_values(h, hb, g):
                G, b = 4 * h + g, g % 2
                wait(eng, s_raw_read, 8 * h + 2 * g + 2)
                wait(eng, s_v_high, G + 1)
                v = V[:, hb, 4 * g:4 * g + 4, :]
                eng.tensor_tensor(v[:, :, DH + 1:2 * DH + 1], raw[:, g, :, 2 * DH:QKV], v[:, :, 0:DH],
                                  ALU.subtract).then_inc(s_v_low, 1)

            def low_parts(h, hb, g):
                G, b = 4 * h + g, g % 2
                wait(eng, s_qk_high, G + 1)
                both = stk[:, g, :, 0:4 * DH].rearrange("p t (k x) -> p t k x", k=2)
                eng.tensor_tensor(both[:, :, :, DH:2 * DH], nrm[:, b, :, :, :], both[:, :, :, 0:DH],
                                  ALU.subtract).then_inc(s_qk_low, 1)

            def prepare(h, hb, s):
                if (g := at_slot(SUM_AT.__getitem__, s, 4)) is not None:
                    inverse_norms(h, hb, g)
                    low_values(h, hb, g)
                if (g := at_slot(NORM_AT.__getitem__, s, 4)) is not None:
                    low_parts(h, hb, g)

            def slot(i, s):
                h, sh = 2 * i + s // SLOTS, s % SLOTS
                if not ended(i) and sh in POOL_LO:
                    low_probs(i, s)
                if prepares(i, s):
                    prepare(h + 1, (s // SLOTS + 1) % 2, sh)
                if s % 2 == 0:
                    if s >= 4 and not ended(i):
                        divide(i, s - 4)
                    elif s < 4 and started(i, 1):
                        divide(i - 1, s + 2 * SLOTS - 4)

            for m in (t["ident16"], t["ident32"]):
                eng.memset(m[:, :], 0.0).then_inc(s_ident, 1)
            eng.memset(half[:, :], -0.5).then_inc(s_half, 1)
            eng.wait_ge(s_ident, 2)
            for m in (t["ident16"], t["ident32"]):
                eng.affine_select(out=m[:, :], in_=m[:, :], compare_op=ALU.not_equal, fill=1.0, base=0,
                                  pattern=[[-1, P]], channel_multiplier=1).then_inc(s_ident, 1)
            eng.wait_ge(s_half, 1)
            inverse_norms(0, 0, 0)
            for g in range(4):
                if g < 3:
                    inverse_norms(0, 0, g + 1)
                low_values(0, 0, g)
                low_parts(0, 0, g)
            heads(eng, slot, constants.gpsimd)

    sem.end()


TB = NT // B
G2 = 2
TG = S // G2


class Turn:

    def __init__(self, t, jobs, sb, sem, YT, XT):
        self.t, self.jobs, self.YT, self.XT = t, jobs, YT, XT
        self.stats = sb("stats", [P, B, TB, 6], F32)
        self.mv = sb("mv", [P, B, TB, 2], F32)
        self.ve = sb("ve", [P, B, TB], F32)
        self.rstd = sb("rstd", [P, B, TB], F32)
        (self.s_addend, self.s_added, self.s_stats, self.s_mv, self.s_ve, self.s_rstd, self.s_rows, self.s_turned,
         self.s_xT, self.s_xl, self.s_out) = (
            sem("t_" + n) for n in ("addend", "added", "stats", "mv", "ve", "rstd", "rows", "turned", "xT", "xl", "out"))

    def stores(self, eng):
        t = self.t
        for n, (b, _, store) in enumerate(self.jobs):
            if store is not None:
                rows = store.rearrange("(t p) d -> p t d", p=P)
                for k in range(0, TB, TB // 2):
                    eng.wait_ge(self.s_rows, TB * n + k + TB // 2)
                    eng.dma_start(rows[:, k:k + TB // 2, :],
                                  t["x"][:, TB * b + k:TB * b + k + TB // 2, :]).then_inc(self.s_out, 16)

    def stores_end(self, eng):
        if self.jobs[-1][2] is not None:
            eng.wait_ge(self.s_out, 32)

    def turned(self, n):
        return n < len(self.jobs) and self.jobs[n][2] is None

    def addend(self, eng):
        b, adds, _ = self.jobs[0]
        if adds:
            for k in range(2):
                for r in range(4):
                    mm = eng.transpose(self.YT[k][:, r, :], self.t[adds][:, b, (4 * k + r) * P:(4 * k + r + 1) * P],
                                       self.t["ident32"][:, :])
                mm.then_inc(self.s_addend, 1)

    def transposes(self, eng, n):
        b = self.jobs[n][0]
        for k in range(2):
            eng.wait_ge(self.s_rows, TB * n + 4 * k + 4)
            for r in range(4):
                mm = eng.transpose(self.XT[2 * n + k][:, r, :], self.t["x"][:, TB * b + 4 * k + r, :],
                                   self.t["ident32"][:, :])
            mm.then_inc(self.s_turned, 1)

    def read(self, eng, n):
        b = self.jobs[n][0]
        for k in range(2):
            eng.wait_ge(self.s_turned, 2 * n + k + 1)
            col = b * S + 4 * k * P
            eng.activation(self.t["xT"][:, col:col + 4 * P], self.XT[2 * n + k][:, :, :].rearrange("p r c -> p (r c)"),
                           ACT.Copy).then_inc(self.s_xT, 1)

    def inverse_deviations(self, eng):
        for n, (b, _, _) in enumerate(self.jobs):
            for k in range(2):
                tiles = slice(TB // 2 * k, TB // 2 * (k + 1))
                eng.wait_ge(self.s_ve, 2 * n + k + 1)
                eng.tensor_tensor(self.rstd[:, b, tiles], self.ve[:, b, tiles],
                                  self.t["half"][:, 0:1].to_broadcast([P, TB // 2]), ALU.pow).then_inc(self.s_rstd, 1)

    def statistics(self, eng, n):
        b, adds, _ = self.jobs[n]
        x = self.t["x"]
        for half in range(2):
            tiles = range(TB // 2 * half, TB // 2 * (half + 1))
            if adds:
                eng.wait_ge(self.s_addend, half + 1)
                xs = x[:, TB * b + tiles[0]:TB * b + tiles[-1] + 1, :]
                eng.tensor_tensor(xs, xs, self.YT[half][:, :, :], ALU.add).then_inc(self.s_added, 1)
                eng.wait_ge(self.s_added, half + 1)
            for k in tiles:
                eng.bn_stats(self.stats[:, b, k, :], x[:, TB * b + k, :]).then_inc(self.s_stats, 1)
            for k in tiles:
                eng.wait_ge(self.s_stats, TB * n + k + 1)
                eng.bn_aggr(self.mv[:, b, k, :], self.stats[:, b, k, :]).then_inc(self.s_mv, 1)
            eng.wait_ge(self.s_mv, TB * n + tiles[-1] + 1)
            eng.tensor_scalar(self.ve[:, b, tiles[0]:tiles[-1] + 1], self.mv[:, b, tiles[0]:tiles[-1] + 1, 1], EPS, None,
                              ALU.add).then_inc(self.s_ve, 1)

    def rows(self, eng, n):
        b = self.jobs[n][0]
        for k in range(TB):
            if k % (TB // 2) == 0:
                eng.wait_ge(self.s_rstd, 2 * n + k // (TB // 2) + 1)
            xs = self.t["x"][:, TB * b + k, :]
            eng.tensor_scalar(xs, xs, self.mv[:, b, k, 0:1], self.rstd[:, b, k:k + 1], ALU.subtract,
                              ALU.mult).then_inc(self.s_rows, 1)

    def low(self, eng):
        b = self.jobs[0][0]
        for k in range(2):
            eng.wait_ge(self.s_xT, k + 1)
            cols = slice(b * S + 4 * k * P, b * S + 4 * (k + 1) * P)
            xs = self.t["xT"][:, cols]
            eng.tensor_tensor(self.t["xl"][:, cols], xs, high(xs)[:, 1::2], ALU.subtract).then_inc(self.s_xl, 1)


def last_rows(nc, tag, t, jobs):
    es = ExitStack()
    sem = Semaphores(nc, tag)
    with es:
        def sb(name, shape, dt):
            return es.enter_context(nc.sbuf_tensor(f"{name}_{tag}", shape, dt))

        turn = Turn(t, jobs, sb, sem, None, None)
        block = es.enter_context(nc.Block())

        @block.sync
        def _(eng):
            turn.stores(eng)
            turn.stores_end(eng)

        @block.gpsimd
        def _(eng):
            turn.inverse_deviations(eng)

        @block.vector
        def _(eng):
            for n in range(len(jobs)):
                turn.statistics(eng, n)
                turn.rows(eng, n)

    sem.end()


def experts(nc, tag, t, io, layer, b, ssm, jobs, following=None, first=0):
    NE = E + layer
    W = (3, 2)[layer] * FF
    DOWN = (2, 1)[layer] * FF
    es = ExitStack()
    sem = Semaphores(nc, tag)
    with es:
        def sb(name, shape, dt):
            return es.enter_context(nc.sbuf_tensor(f"{name}_{tag}", shape, dt))

        x, xT, xl, cw = t["x"], t["xT"], t["xl"], t["cw"]
        wf, wh, wl = (lambda k, n=n: t[n][:, (k + first) % 2, 0:W] for n in ("wf", "wh", "wl"))
        act = sb("act", [P, NC, TG], F32)
        hid = sb("hid", [P, 2, NC, TG], F32)
        hlo = sb("hlo", [P, 2, NC, TG], F16)
        GB = [es.enter_context(nc.psum_tensor(f"GB{i}_{tag}", [P, TG], F32)) for i in range(2)]
        UB = [es.enter_context(nc.psum_tensor(f"UB{i}_{tag}", [P, TG], F32)) for i in range(4)]
        DB = [es.enter_context(nc.psum_tensor(f"DB{i}_{tag}", [P, 4, P], F32)) for i in range(2)]
        FB = GB if layer == 0 else UB
        NF = len(FB)
        lg = sb("lg", [P, TB, E], F32)
        mx = sb("mx", [P, TB, 8], F32)
        ix = sb("ix", [P, TB, 8], U32)
        ixf = sb("ixf", [P, TB, 2], F32)
        df, ex, e1, p1, p2 = (sb(n, [P, TB], F32) for n in ("df", "ex", "e1", "p1", "p2"))
        m1, m2 = sb("m1", [P, TB, E], F32), sb("m2", [P, TB, E], F32)
        if ssm is not None:
            xf = sb("xf", [P, S], F32)
            sg = sb("sg", [P, S], F32)
            dt = sb("dt", [P, S], F32)
            us = sb("us", [P, S], F32)
            ea = sb("ea", [P, 2, S], F32)
            bu = sb("bu", [P, 2, S], F32)
            st = sb("st", [P, 2, S], F32)

        s_w_loaded = [sem(f"w{i}") for i in range(2)]
        s_next_loaded = [sem(f"next{i}") for i in range(2)]

        def place(name, e):
            return t[name][:, (e + first) % 2, 0:(3, 2)[following] * FF]

        def beyond(i, k):
            return isinstance(i, int) and 2 * i + k >= NE

        (s_w_high, s_w_low, s_up_products, s_activated, s_hidden, s_hidden_low, s_down_products, s_added) = (
            sem(n) for n in ("w_high", "w_low", "up", "activated", "hidden", "hidden_low", "down", "added"))
        (s_convolved, s_step_products, s_sigmoids, s_steps, s_step_inputs, s_decays, s_state_inputs, s_states,
         s_state_sums) = (
            sem(n) for n in ("convolved", "step_products", "sigmoids", "steps", "step_inputs", "decays",
                             "state_inputs", "states", "state_sums"))
        (s_logits, s_logits_read, s_largest, s_indices, s_differences, s_exp, s_denominator, s_first_weight,
         s_second_weight, s_one_hot, s_weighted, s_expert_weights) = (
            sem(n) for n in ("logits", "logits_read", "largest", "indices", "differences", "exp", "denominator",
                             "first_weight", "second_weight", "one_hot", "weighted", "expert_weights"))
        turned_banks = [bank[:, :].rearrange("p (r c) -> p r c", r=4) for bank in UB[2:]]
        turn = Turn(t, jobs, sb, sem, DB, (turned_banks[0], turned_banks[1], DB[0], DB[1]))
        block = es.enter_context(nc.Block())

        def group(i, k, g):
            return 2 * k + g if isinstance(i, int) and i == 0 else None

        w_io = io[f"w{layer}"]

        def each(eng, emit, end=None):
            for k in range(2):
                emit(0, k)
            with eng.Fori(1, (NE - 1) // 2) as i:
                for k in range(2):
                    emit(i, k)
            for e in range(2 * ((NE - 1) // 2), NE):
                emit(e // 2, e % 2)
            if end:
                end()

        def states(i, k, g):
            if ssm is None or group(i, k, g) in (0, 1):
                return ()
            if layer:
                return ((i, g),) if k else ((i - 1, 2 + g),)
            return tuple((0, 2 * g + m) for m in range(2)) if group(i, k, g) else ((i, 2 * k + g),)

        @block.sync
        def _(eng):
            def load(i, k):
                if isinstance(i, int) and i == 0:
                    return
                wait(eng, s_w_high, 2 * i + k - 2)
                wait(eng, s_w_low, 2 * i + k - 2)
                eng.dma_start(wf(k), w_io[:, bass.ds(W * (2 * i + k), W)]).then_inc(s_w_loaded[k], 16)

            turn.stores(eng)
            each(eng, load)
            if following is not None:
                for k in range(2):
                    eng.wait_ge(s_w_high, NE - 2 + k)
                    eng.wait_ge(s_w_low, NE - 2 + k)
                    size = (3, 2)[following] * FF
                    eng.dma_start(place("wf", NE + k), io[f"w{following}"][:, size * k:size * k + size]).then_inc(
                        s_next_loaded[k], 16)
                eng.wait_ge(s_next_loaded[1], 16)
            turn.stores_end(eng)

        @block.tensor
        def _(eng):
            def unit(i, k, g, c):
                U = 16 * i + 8 * k + 4 * g + c
                e = 2 * i + k
                if g == 0 and c == 0:
                    wait(eng, s_w_high, e)
                    wait(eng, s_w_low, e)
                wait(eng, s_activated, U - NF + 1)
                if layer == 0:
                    wait(eng, s_hidden, U - 3)
                if group(i, k, g) == 0 and c in (0, 3):
                    eng.wait_ge(turn.s_xT, 1 if c == 0 else 2)
                    eng.wait_ge(turn.s_xl, 1)
                if group(i, k, g) == 1:
                    eng.wait_ge(turn.s_xl, 2)
                col = b * S + g * TG
                xh, xlo = high(xT[:, col:col + TG])[:, 1::2], xl[:, col:col + TG]
                for m, bank in enumerate((FB[c % NF], UB[c])[:2 - layer]):
                    at = m * FF + P * c
                    eng.matmul(bank[:, :], wh(k)[:, at:at + P], xh, start=True, stop=False)
                    eng.matmul(bank[:, :], wl(k)[:, at:at + P], xh, start=False, stop=False)
                    mm = eng.matmul(bank[:, :], wh(k)[:, at:at + P], xlo, start=False, stop=True)
                mm.then_inc(s_up_products, 1)

            def down(i, k, g, tile):
                Q = 4 * i + 2 * k + g
                if tile == 0:
                    if group(i, k, g) == 1:
                        eng.wait_ge(s_logits_read, 1)
                    if ssm is not None and isinstance(i, int) and i == 0:
                        eng.wait_ge(s_sigmoids, 2)
                    wait(eng, s_hidden_low, 4 * Q + 4)
                    wait(eng, s_added, 4 * (Q - 1))
                for c in range(NC):
                    h = high(hid[:, g, c, P * tile:P * tile + P])[:, 1::2]
                    hl = hlo[:, g, c, P * tile:P * tile + P]
                    at = DOWN + P * c
                    out = DB[g][:, tile, :]
                    eng.matmul(out, h, wh(k)[:, at:at + P], start=c == 0, stop=False)
                    eng.matmul(out, h, wl(k)[:, at:at + P], start=False, stop=False)
                    mm = eng.matmul(out, hl, wh(k)[:, at:at + P], start=False, stop=c == NC - 1)
                if tile == 3:
                    mm.then_inc(s_down_products, 1)

            def before(i, k, g):
                if g:
                    return i, k, 0
                if k:
                    return i, 0, 1
                return None if isinstance(i, int) and i == 0 else (i - 1, 1, 1)

            def expert(i, k):
                for g in range(2):
                    for c in range(NC):
                        unit(i, k, g, c)
                        if group(i, k, g) == 0 and c == 2 and turn.turned(1):
                            turn.transposes(eng, 1)
                        if ssm is not None and group(i, k, g) == 1 and c == 1:
                            step_products()
                        late = layer or ssm is not None and group(i, k, g) == 1
                        if c == (3 if late else 1) and (q := before(i, k, g)):
                            for tile in range(4):
                                down(*q, tile)
                    if group(i, k, g) == (1 if turn.turned(1) else 0):
                        logits()

            def end():
                for tile in range(4):
                    down(*((E // 2 - 1, 1, 1) if NE == E else (E // 2, 0, 1)), tile)

            def logits():
                if ssm is not None:
                    eng.wait_ge(s_sigmoids, 2)
                for k in range(TB):
                    mm = eng.matmul(DB[1][:, 0, E * k:E * k + E], xT[:, b * S + k * P:b * S + (k + 1) * P],
                                    t[("gate", "router")[layer]][:, :], start=True, stop=True)
                mm.then_inc(s_logits, 1)

            def step_products():
                eng.wait_ge(s_convolved, 3)
                for m in range(2):
                    eng.matmul(DB[m][:, :, :].rearrange("p a b -> p (a b)"), t["dtw"][:, :], xf[:, m * TG:m * TG + TG], start=True,
                               stop=True).then_inc(s_step_products, 1)
            turn.addend(eng)
            turn.transposes(eng, 0)
            each(eng, expert, end)

        @block.scalar
        def _(eng):
            def unit(i, k, g, c):
                U = 16 * i + 8 * k + 4 * g + c
                Q = 4 * i + 2 * k + g
                wait(eng, s_up_products, U + 1)
                if layer == 0:
                    wait(eng, s_hidden, U - 3)
                    eng.activation(act[:, c, :], FB[c % NF][:, :], ACT.Silu).then_inc(s_activated, 1)
                else:
                    wait(eng, s_hidden, U - 3)
                    eng.activation(act[:, c, :], FB[c % NF][:, :], ACT.Relu).then_inc(s_activated, 1)
                    wait(eng, s_activated, U + 1)
                    if c == 0:
                        wait(eng, s_down_products, Q - 1)
                    eng.activation(hid[:, g, c, :], act[:, c, :], ACT.Square).then_inc(s_hidden, 1)

            def state(i, d):
                n = 4 * i + d
                wait(eng, s_steps, 1)
                wait(eng, s_states, n - 1)
                eng.activation(ea[:, d % 2, :], dt[:, :], ACT.Exp, scale=t["A"][:, bass.ds(n, 1)]).then_inc(
                    s_decays, 1)

            def expert(i, k):
                for g in range(2):
                    for c in range(NC):
                        unit(i, k, g, c)
                        if group(i, k, g) == 0 and c == 2 and turn.turned(1):
                            turn.read(eng, 1)
                        if ssm is not None and group(i, k, g) == 1 and c == 1:
                            for m in range(2):
                                eng.wait_ge(s_step_products, m + 1)
                                eng.activation(sg[:, m * TG:m * TG + TG], DB[m][:, :, :].rearrange("p a b -> p (a b)"),
                                               ACT.Sigmoid, bias=t["dtb"][:, 0:1]).then_inc(s_sigmoids, 1)
                        if c == (1, 3)[layer]:
                            for j, d in states(i, k, g):
                                state(j, d)
                    if group(i, k, g) == 1:
                        eng.wait_ge(s_differences, 1)
                        eng.activation(ex[:, :], df[:, :], ACT.Exp).then_inc(s_exp, 1)

            turn.read(eng, 0)
            each(eng, expert)

        @block.vector
        def _(eng):
            def split(i, k):
                e = 2 * i + k
                wait(eng, s_down_products, 2 * (e - 1))
                if beyond(i, k):
                    eng.wait_ge(s_next_loaded[0], 16)
                    eng.tensor_copy(place("wh", e), place("wf", e)).then_inc(s_w_high, 1)
                    return
                wait(eng, s_w_loaded[k], 16 * i)
                eng.tensor_copy(wh(k), wf(k)).then_inc(s_w_high, 1)

            def unit(i, k, g, c):
                U = 16 * i + 8 * k + 4 * g + c
                Q = 4 * i + 2 * k + g
                h = hid[:, g, c, :]
                if layer == 0:
                    wait(eng, s_activated, U + 1)
                    if c == 0:
                        wait(eng, s_down_products, Q - 1)
                    eng.tensor_tensor(h, act[:, c, :], UB[c][:, :], ALU.mult).then_inc(s_hidden, 1)
                    wait(eng, s_hidden, U + 1)
                else:
                    wait(eng, s_hidden, U + 1)
                eng.tensor_tensor(hlo[:, g, c, :], h, high(h)[:, 1::2], ALU.subtract).then_inc(s_hidden_low, 1)

            def add(i, k, g):
                Q = 4 * i + 2 * k + g
                e = 2 * i + k
                wait(eng, s_down_products, Q + 1)
                for tile in range(4):
                    xs = x[:, TB * b + 4 * g + tile, :]
                    eng.scalar_tensor_tensor(out=xs, in0=DB[g][:, tile, :],
                                             scalar=cw[:, TB * b + 4 * g + tile, bass.ds(e, 1)], in1=xs,
                                             op0=ALU.mult, op1=ALU.add).then_inc(s_added, 1)

            def choose():
                eng.wait_ge(s_logits, 1)
                eng.tensor_copy(lg[:, :, :], DB[1][:, 0, 0:TB * E].rearrange("p (k e) -> p k e", e=E)).then_inc(
                    s_logits_read, 1)
                eng.wait_ge(s_logits_read, 1)
                for k in range(TB):
                    eng.max(mx[:, k, :], lg[:, k, :]).then_inc(s_largest, 1)
                eng.wait_ge(s_largest, TB)
                eng.tensor_tensor(df[:, :], mx[:, :, 1], mx[:, :, 0], ALU.subtract).then_inc(s_differences, 1)
                for k in range(TB):
                    eng.max_index(ix[:, k, :], mx[:, k, :], lg[:, k, :]).then_inc(s_indices, 1)
                eng.wait_ge(s_indices, TB)
                eng.tensor_copy(ixf[:, :, :], ix[:, :, 0:2]).then_inc(s_indices, 1)

            def combine():
                eng.wait_ge(s_exp, 1)
                eng.tensor_scalar(e1[:, :], ex[:, :], 1.0, None, ALU.add).then_inc(s_denominator, 1)
                eng.wait_ge(s_indices, TB + 1)
                iota = t["iota"][:, :].unsqueeze(1).to_broadcast([P, TB, E])
                for k, m in enumerate((m1, m2)):
                    eng.tensor_tensor(m[:, :, :], iota, ixf[:, :, k:k + 1].to_broadcast([P, TB, E]),
                                      ALU.is_equal).then_inc(s_one_hot, 1)
                eng.wait_ge(s_denominator, 1)
                eng.reciprocal(p1[:, :], e1[:, :]).then_inc(s_first_weight, 1)
                eng.wait_ge(s_first_weight, 1)
                eng.tensor_tensor(p2[:, :], ex[:, :], p1[:, :], ALU.mult).then_inc(s_second_weight, 1)
                eng.wait_ge(s_second_weight, 1)
                eng.wait_ge(s_one_hot, 2)
                for m, pr in ((m1, p1), (m2, p2)):
                    eng.tensor_tensor(m[:, :, :], m[:, :, :], pr[:, :].unsqueeze(2).to_broadcast([P, TB, E]),
                                      ALU.mult).then_inc(s_weighted, 1)
                eng.wait_ge(s_weighted, 2)
                eng.tensor_tensor(cw[:, TB * b:TB * b + TB, 0:E], m1[:, :, :], m2[:, :, :], ALU.add).then_inc(
                    s_expert_weights, 1)
                eng.wait_ge(s_expert_weights, 1)

            def convolve():
                eng.wait_ge(turn.s_xT, 4)
                xs = xT[:, ssm * S:ssm * S + S]
                eng.tensor_scalar(xf[:, :], xs, t["cvw"][:, 1:2], t["cvb"][:, 0:1], ALU.mult, ALU.add).then_inc(
                    s_convolved, 1)
                eng.wait_ge(s_convolved, 1)
                eng.scalar_tensor_tensor(out=xf[:, 1:S], in0=xs[:, 0:S - 1], scalar=t["cvw"][:, 0:1], in1=xf[:, 1:S],
                                         op0=ALU.mult, op1=ALU.add).then_inc(s_convolved, 1)
                eng.wait_ge(s_convolved, 2)
                eng.scalar_tensor_tensor(out=xf[:, 0:S - 1], in0=xs[:, 1:S], scalar=t["cvw"][:, 2:3],
                                         in1=xf[:, 0:S - 1], op0=ALU.mult, op1=ALU.add).then_inc(s_convolved, 1)

            def steps():
                eng.wait_ge(s_sigmoids, 2)
                eng.tensor_scalar(dt[:, :], sg[:, :], 0.1 - 0.001, 0.001, ALU.mult, ALU.add).then_inc(s_steps, 1)
                eng.wait_ge(s_steps, 1)
                eng.tensor_tensor(us[:, :], dt[:, :], xf[:, :], ALU.mult).then_inc(s_step_inputs, 1)

            def scan(i, d):
                n = 4 * i + d
                wait(eng, s_state_inputs, n + 1)
                wait(eng, s_decays, n + 1)
                wait(eng, s_state_sums, n)
                eng.tensor_tensor_scan(st[:, d % 2, :], ea[:, d % 2, :], bu[:, d % 2, :], 0.0, ALU.mult,
                                       ALU.add).then_inc(s_states, 1)

            def expert(i, k):
                for g in range(2):
                    for c in range(NC):
                        if c == 0 and g == 1:
                            if following is not None or not beyond(i + k, 1 - k):
                                split(i + k, 1 - k)
                        unit(i, k, g, c)
                        if group(i, k, g) == 0 and c == 2 and ssm is not None:
                            convolve()
                        if group(i, k, g) == 1 and c == 3 and ssm is not None:
                            steps()
                        if group(i, k, g) == 1 and c == 1 and not turn.turned(1):
                            choose()
                        if group(i, k, g) == 2 and c == 0:
                            combine()
                        if c == 1 and (q := expert_before(i, k, g)):
                            add(*q)
                        if c == 3:
                            for j, d in states(i, k, g):
                                scan(j, d)
                    if group(i, k, g) == 1 and turn.turned(1):
                        choose()

            def expert_before(i, k, g):
                if k:
                    return i, 0, g
                return None if isinstance(i, int) and i == 0 else (i - 1, 1, g)

            def last():
                for g in range(2):
                    add(*((E // 2 - 1, 1, g) if NE == E else (E // 2, 0, g)))

            turn.statistics(eng, 0)
            turn.rows(eng, 0)
            turn.low(eng)
            if len(jobs) > 1:
                turn.statistics(eng, 1)
                turn.rows(eng, 1)
            each(eng, expert, last)

        @block.gpsimd
        def _(eng):
            def split(i, k):
                e = 2 * i + k
                wait(eng, s_w_high, e)
                parts = [place(n, e) for n in ("wl", "wf", "wh")] if beyond(i, k) else (wl(k), wf(k), wh(k))
                eng.tensor_tensor(*parts, ALU.subtract).then_inc(s_w_low, 1)

            def inputs(i, d):
                n = 4 * i + d
                wait(eng, s_step_inputs, 1)
                wait(eng, s_states, n - 1)
                eng.tensor_tensor(bu[:, d % 2, :], us[:, :], t["bc"][:, bass.ds(n, 1)].to_broadcast([P, S]),
                                  ALU.mult).then_inc(s_state_inputs, 1)

            def sum_state(i, d):
                n = 4 * i + d
                wait(eng, s_states, n + 1)
                y = t["y"][:, ssm, :]
                wait(eng, s_state_sums, n + 1)
                eng.tensor_tensor(y, y, st[:, d % 2, :], ALU.add).then_inc(s_state_sums, 1)

            def expert(i, k):
                for g in range(2):
                    if g == 1:
                        if following is not None or not beyond(i + k, 1 - k):
                            split(i + k, 1 - k)
                    for j, d in states(i, k, g):
                        inputs(j, d)
                        if d:
                            sum_state(j, d - 1)
                        elif not (isinstance(j, int) and j == 0):
                            sum_state(j - 1, 3)

            def last_sum():
                if ssm is not None:
                    sum_state(DS // 4 - 1, 3)

            if ssm is not None:
                eng.memset(t["y"][:, ssm, :], 0.0).then_inc(s_state_sums, 1)
            turn.inverse_deviations(eng)
            each(eng, expert, last_sum)

    sem.end()


def program(nc, io, out):
    ctx = ExitStack()
    with ctx:
        def sb(name, shape, dt):
            return ctx.enter_context(nc.sbuf_tensor(name, shape, dt))

        t = {
            "x": sb("x", [P, NT, D], F32),
            "ident16": sb("ident16", [P, P], F16),
            "ident32": sb("ident32", [P, P], F32),
            "half": sb("half", [P, 1], F32),
            "wf": sb("wf", [P, 2, 3 * FF], F32),
            "wh": sb("wh", [P, 2, 3 * FF], F16),
            "wl": sb("wl", [P, 2, 3 * FF], F16),
            "cw": sb("cw", [P, NT, E + 1], F32),
            "iota": sb("iota", [P, E], F32),
            "gate": sb("gate", [P, E], F32),
            "router": sb("router", [P, E], F32),
            "dtw": sb("dtw", [P, D], F32),
            "dtb": sb("dtb", [P, 1], F32),
            "cvw": sb("cvw", [P, 3], F32),
            "cvb": sb("cvb", [P, 1], F32),
            "A": sb("A", [P, DS], F32),
            "bc": sb("bc", [P, DS], F32),
        }
        attention(nc, io, t)
        t |= {
            "xT": sb("xT", [P, T], F32),
            "xl": sb("xl", [P, T], F16),
            "y": sb("y", [P, B, S], F32),
        }
        experts(nc, "e1", t, io, 0, 0, None, ((0, None, None),), 0)
        experts(nc, "e2", t, io, 0, 1, 0, ((1, None, None), (0, None, None)), 1)
        experts(nc, "e3", t, io, 1, 0, 1, ((0, "y", None), (1, None, None)), 1)
        experts(nc, "e4", t, io, 1, 1, None, ((1, "y", None), (0, None, out[0])), first=1)
        last_rows(nc, "r", t, ((1, None, out[1]),))


def layout(inputs):
    import numpy as np
    a = {k: np.asarray(v) for k, v in inputs.items()}
    x = a["L0_attn_x"].reshape(T, D)
    wq = a["L0_attn_w_q"].reshape(D, H, DH)
    wkv = a["L0_attn_w_kv"].reshape(D, 2, H, DH)

    def up(w):
        return w.transpose(2, 0, 1)

    def down(w):
        return w.reshape(-1, D, NC, P).transpose(3, 0, 2, 1).reshape(P, -1, NC * D)

    w_fc = np.concatenate([a["L1_ffn_w_fc"], a["L1_ffn_shared_fc"][None]])
    w_proj = np.concatenate([a["L1_ffn_w_proj"], a["L1_ffn_shared_proj"][None]])
    named = {
        "x": x,
        "xT": x.T,
        "wqkv": np.concatenate([wq, wkv[:, 0], wkv[:, 1]], axis=2).reshape(D, H * QKV),
        "wout": a["L0_attn_w_out"].reshape(H // 2, P, D).transpose(1, 0, 2).reshape(P, H // 2 * D),
        "b_out": a["L0_attn_b_out"],
        "scale": a["L0_attn_scale"].reshape(H),
        "w0": np.concatenate([up(a["L0_ffn_wg"]), up(a["L0_ffn_wu"]), down(a["L0_ffn_wd"])], axis=2).reshape(P, -1),
        "w1": np.concatenate([up(w_fc), down(w_proj)], axis=2).reshape(P, -1),
        "gateT": a["L0_ffn_gate_w"].T,
        "routerT": a["L1_ffn_router_w"].T,
        "a_log": a["L1_attn_a_log"],
        "b": a["L1_attn_b"],
        "c": a["L1_attn_c"],
        "dtwT": a["L1_attn_dt_w"].T,
        "dt_b": a["L1_attn_dt_b"].reshape(D, 1),
        "conv_w": a["L1_attn_conv_w"].reshape(D, 3),
        "conv_b": a["L1_attn_conv_b"].reshape(D, 1),
    }
    return {k: np.ascontiguousarray(v) for k, v in named.items()}


def kernel(**inputs):
    import numpy as np
    import concourse.bacc as bacc
    from concourse.bass_utils import run_bass_kernel_spmd as run

    nc = bacc.Bacc("TRN2", target_bir_lowering=False, num_devices=1)
    arrays = {f"in_{k}": v for k, v in layout(inputs).items()}
    io = {k[3:]: nc.dram_tensor(k, a.shape, mybir.dt.from_np(a.dtype), kind="ExternalInput").ap()
          for k, a in arrays.items()}
    out = nc.dram_tensor("out", (B, S, D), F32, kind="ExternalOutput").ap()
    program(nc, io, out)
    return run(nc, [arrays], core_ids=[0]).results[0]["out"]
```
